# Optimizing a Trainium2 kernel written in Bass

```python
import numpy as np
import jax
import jax.numpy as jnp

def _softmax(x, axis=-1):
    return jax.nn.softmax(x, axis=axis)

def _gelu(x):
    return jax.nn.gelu(x, approximate=True)

def _silu(x):
    return jax.nn.silu(x)

def _sigmoid(x):
    return jax.nn.sigmoid(x)

def _layernorm(x, axis=-1, eps=1e-05):
    m = jnp.mean(x, axis=axis, keepdims=True)
    v = jnp.var(x, axis=axis, keepdims=True)
    return (x - m) / jnp.sqrt(v + eps)

def _scatter_add(tgt, idx, src, axis=0):
    return tgt.at[idx].add(src)

def _segment_sum(src, seg, n):
    return jax.ops.segment_sum(src, seg, n)
kernel_name = 'mk_adj_ffn_d1_adj_r2_d35f52'

def setup_inputs(seed: int=0):
    np.random.seed(seed)
    _w = jnp.asarray

    def _rec_inputs():
        import jax
        import jax.numpy as jnp
        _gk = jax.random.key(seed)
        x = -0.001547 + 1.001 * jax.random.normal(jax.random.fold_in(_gk, 1), (512, 128), jnp.float32)
        _w = (1.0 + jnp.arange(512, dtype=jnp.float32)) ** (-0.5)
        _w = _w / _w.mean()
        _pij = jnp.clip(0.03125 * _w[:, None] * _w[None, :], 0.0, 1.0)
        _a = jax.random.uniform(jax.random.fold_in(_gk, 2), (512, 512)) < _pij
        adj = _a.astype(jnp.int32)
        return (x, adj)
    x, adj = _rec_inputs()

    def _L0_gnn_setup():
        import jax, jax.numpy as jnp
        import numpy as np
        BT, BN, D, H = (512, 512, 128, 8)
        DH = D // H
        key = jax.random.key(seed)
        ks = jax.random.split(key, 16)
        s = 1.0 / np.sqrt(D)
        return {'h_target': jax.random.normal(ks[0], (BT, D), jnp.float32), 'h_neigh': jax.random.normal(ks[1], (BN, D), jnp.float32), 'adjacency': jax.random.randint(ks[2], (BT, BN), 0, 2, jnp.int32), 'edge_types': jax.random.randint(ks[3], (BT, BN), 0, 2, jnp.int32), 'Wq': jax.random.normal(ks[4], (D, D), jnp.float32) * s, 'bq': jnp.zeros((D,), jnp.float32), 'Wk': jax.random.normal(ks[5], (D, D), jnp.float32) * s, 'bk': jnp.zeros((D,), jnp.float32), 'Wv': jax.random.normal(ks[6], (D, D), jnp.float32) * s, 'bv': jnp.zeros((D,), jnp.float32), 'Wo': jax.random.normal(ks[7], (D, D), jnp.float32) * s, 'bo': jnp.zeros((D,), jnp.float32), 'E': jax.random.normal(ks[8], (2, D), jnp.float32)}
    _L0_gnn_all = _L0_gnn_setup()
    _L0_gnn_in = {k: v for k, v in _L0_gnn_all.items() if k in ('h_neigh', 'Wq', 'bq', 'Wk', 'bk', 'Wv', 'bv', 'Wo', 'bo', 'E')}
    del _L0_gnn_all

    def _L0_ffn_setup():
        import jax, jax.numpy as jnp
        import numpy as np
        B, T, IN_DIM = (64, 128, 128)
        HID, OUT_DIM = (256, 128)
        N_LAYERS, N_EXPERTS, N_SHARED = (2, 16, 1)
        key = jax.random.key(seed)
        ks = jax.random.split(key, 10)
        s = 0.02
        x = jax.random.normal(ks[0], (B, T, IN_DIM), dtype=jnp.float32)
        route_id = jax.random.randint(ks[1], (B,), 0, N_EXPERTS)
        Wi = jax.random.normal(ks[2], (HID, IN_DIM), dtype=jnp.float32) * s
        bi = jnp.zeros((HID,), dtype=jnp.float32)
        Wr = jax.random.normal(ks[3], (N_LAYERS, N_EXPERTS, HID, HID), dtype=jnp.float32) * s
        br = jax.random.normal(ks[4], (N_LAYERS, N_EXPERTS, HID), dtype=jnp.float32) * s
        Ws = jax.random.normal(ks[5], (N_LAYERS, N_SHARED, HID, HID), dtype=jnp.float32) * s
        bs = jax.random.normal(ks[6], (N_LAYERS, N_SHARED, HID), dtype=jnp.float32) * s
        Wo = jax.random.normal(ks[7], (OUT_DIM, HID), dtype=jnp.float32) * s
        bo = jnp.zeros((OUT_DIM,), dtype=jnp.float32)
        return {'x': x, 'route_id': route_id, 'Wi': Wi, 'bi': bi, 'Wr': Wr, 'br': br, 'Ws': Ws, 'bs': bs, 'Wo': Wo, 'bo': bo}
    _L0_ffn_all = _L0_ffn_setup()
    _L0_ffn_in = {k: v for k, v in _L0_ffn_all.items() if k in ('route_id', 'Wi', 'bi', 'Wr', 'br', 'Ws', 'bs', 'Wo', 'bo')}
    del _L0_ffn_all
    return {'x': x, 'adj': adj, 'L0_gnn_h_neigh': _L0_gnn_in['h_neigh'], 'L0_gnn_Wq': _L0_gnn_in['Wq'], 'L0_gnn_bq': _L0_gnn_in['bq'], 'L0_gnn_Wk': _L0_gnn_in['Wk'], 'L0_gnn_bk': _L0_gnn_in['bk'], 'L0_gnn_Wv': _L0_gnn_in['Wv'], 'L0_gnn_bv': _L0_gnn_in['bv'], 'L0_gnn_Wo': _L0_gnn_in['Wo'], 'L0_gnn_bo': _L0_gnn_in['bo'], 'L0_gnn_E': _L0_gnn_in['E'], 'L0_ffn_route_id': _L0_ffn_in['route_id'], 'L0_ffn_Wi': _L0_ffn_in['Wi'], 'L0_ffn_bi': _L0_ffn_in['bi'], 'L0_ffn_Wr': _L0_ffn_in['Wr'], 'L0_ffn_br': _L0_ffn_in['br'], 'L0_ffn_Ws': _L0_ffn_in['Ws'], 'L0_ffn_bs': _L0_ffn_in['bs'], 'L0_ffn_Wo': _L0_ffn_in['Wo'], 'L0_ffn_bo': _L0_ffn_in['bo']}

def reference(x, adj, L0_gnn_h_neigh, L0_gnn_Wq, L0_gnn_bq, L0_gnn_Wk, L0_gnn_bk, L0_gnn_Wv, L0_gnn_bv, L0_gnn_Wo, L0_gnn_bo, L0_gnn_E, L0_ffn_route_id, L0_ffn_Wi, L0_ffn_bi, L0_ffn_Wr, L0_ffn_br, L0_ffn_Ws, L0_ffn_bs, L0_ffn_Wo, L0_ffn_bo):
    import jax
    import jax.numpy as jnp

    def _L0_gnn_ref(h_target, h_neigh, adjacency, edge_types, Wq, bq, Wk, bk, Wv, bv, Wo, bo, E):
        import jax, jax.numpy as jnp
        import numpy as np
        BT, BN, D, H = (512, 512, 128, 8)
        DH = D // H
        Bt, d = h_target.shape
        Bn = h_neigh.shape[0]
        msg = h_neigh[None, :, :] + E[edge_types]
        q = (h_target @ Wq.T + bq).reshape(Bt, H, DH)
        k = (msg @ Wk.T + bk).reshape(Bt, Bn, H, DH)
        v = (msg @ Wv.T + bv).reshape(Bt, Bn, H, DH)
        scores = jnp.einsum('bhd,bnhd->bhn', q, k) / np.sqrt(DH).astype(np.float32)
        mask = adjacency[:, None, :] == 0
        scores = jnp.where(mask, jnp.float32(-1000000000.0), scores)
        attn = jax.nn.softmax(scores, axis=-1)
        attn = jnp.where(mask, jnp.float32(0.0), attn)
        out = jnp.einsum('bhn,bnhd->bhd', attn, v).reshape(Bt, d)
        return out @ Wo.T + bo

    def _L0_ffn_ref(x, route_id, Wi, bi, Wr, br, Ws, bs, Wo, bo):
        import jax, jax.numpy as jnp
        import numpy as np
        B, T, IN_DIM = (64, 128, 128)
        HID, OUT_DIM = (256, 128)
        N_LAYERS, N_EXPERTS, N_SHARED = (2, 16, 1)
        flat = x.reshape(-1, x.shape[-1])
        n_tok = flat.shape[0]
        route = jnp.repeat(route_id, n_tok // route_id.shape[0])
        h = jax.nn.relu(flat @ Wi.T + bi)
        n_layers, n_experts = (Wr.shape[0], Wr.shape[1])
        for l in range(n_layers):
            shared = (jnp.einsum('nd,shd->snh', h, Ws[l]) + bs[l][:, None, :]).mean(axis=0)
            routed = jnp.zeros_like(h)
            for e in range(n_experts):
                ye = h @ Wr[l, e].T + br[l, e]
                routed = routed + jnp.where((route == e)[:, None], ye, 0.0)
            h = jax.nn.relu(shared + routed + h)
        out = h @ Wo.T + bo
        return out.reshape(*x.shape[:-1], out.shape[-1])
    x = x + _L0_gnn_ref(_layernorm(x, axis=-1), L0_gnn_h_neigh, adj, adj, L0_gnn_Wq, L0_gnn_bq, L0_gnn_Wk, L0_gnn_bk, L0_gnn_Wv, L0_gnn_bv, L0_gnn_Wo, L0_gnn_bo, L0_gnn_E)
    x = x + _L0_ffn_ref(_layernorm(x, axis=-1)[None], L0_ffn_route_id, L0_ffn_Wi, L0_ffn_bi, L0_ffn_Wr, L0_ffn_br, L0_ffn_Ws, L0_ffn_bs, L0_ffn_Wo, L0_ffn_bo)[0]
    return x

_drawn_inputs = setup_inputs


def setup_inputs(seed=0):
    import zlib

    import numpy as np

    out = dict(_drawn_inputs(seed))
    spreads = {'L0_gnn_bq': (0.0, 0.436),
     'L0_gnn_bk': (0.0, 0.8),
     'L0_gnn_bv': (0.0, 0.1),
     'L0_gnn_bo': (0.0, 0.1),
     'L0_ffn_bi': (0.0, 0.519),
     'L0_ffn_bo': (0.0, 0.1)}
    factors = {'L0_ffn_Wr': 4.065, 'L0_ffn_br': 8.0, 'L0_ffn_Ws': 4.344, 'L0_ffn_bs': 8.0}
    for name, (base, spread) in spreads.items():
        noise = np.random.default_rng([zlib.crc32(name.encode()), seed]).standard_normal(out[name].shape)
        drawn = base * np.exp(spread * noise) if base else spread * noise
        out[name] = jnp.asarray(drawn.astype(out[name].dtype))
    for name, factor in factors.items():
        out[name] = (out[name] * factor).astype(out[name].dtype)
    return out
```

```python
from contextlib import ExitStack

import numpy as np

import concourse.bass as bass
from concourse import mybir

ALU = mybir.AluOpType
ACT = mybir.ActivationFunctionType
F32 = mybir.dt.float32
BF16 = mybir.dt.bfloat16
I32 = mybir.dt.int32

P = 128
N = 512
D = 128
C = N // P
H = 8
DH = D // H
HS = 32
HG = P // HS
G = H // HG
HID = 256
KH = HID // P
L = 2
E = 16
GR = 64
RPG = N // GR
PAIRS = E + C - 1
LAST = PAIRS - C + 1
EPS = 1e-5
NEG = -1e30
FLOOR = -1e15
TINY = 1e-30
MAXBANKS = 3
EXPBANK = 3
OUTBANK = 7
WPARTS = 4

EARLY = {}
LATE = {}


def _columns(table, fields):
    at = 0
    for name, width in fields:
        table[name] = (at, at + width)
        at += width
    return at


EARLY_W = _columns(EARLY, [("ident", P), ("wq", G * P), ("bq", G), ("hnT", N), ("ET", 2),
                           ("wk", G * P), ("bk", G), ("wv", G * P), ("bv", G * P)])
LATE_W = _columns(LATE, [("wo", D), ("bo", D), ("iota", N), ("tile_of", N), ("ones", P), ("row_no", C),
                         ("group_of", C), ("in_group", 1), ("cap", 1), ("wi", HID), ("bi", KH),
                         ("ws", L * KH * HID), ("fwo", KH * D), ("fbo", D)])


def gnn_ffn_kernel(nc, x, early, late, adj, adjT, route_tok, route_row, br, bs, wr, out):
    with ExitStack() as ctx:
        def sb(name, shape, dt=F32):
            return ctx.enter_context(nc.sbuf_tensor(name, shape, dt))

        def sem(name):
            return ctx.enter_context(nc.semaphore(name))

        xs = sb("xs", [P, C, D])
        ea = sb("ea", [P, EARLY_W])
        la = sb("la", [P, LATE_W])
        gather = sb("gather", [P, C, N])
        scatter = sb("scatter", [P, C, N])
        adj_i = gather[:].bitcast(I32)
        adjT_i = scatter[:].bitcast(I32)
        mask = sb("mask", [P, C, N], BF16)
        maskT = sb("maskT", [P, C, N], BF16)
        ident_b = sb("ident_b", [P, P], BF16)
        stats = sb("stats", [P, C, 6])
        mv = sb("mv", [P, C, 2])
        var_eps = sb("var_eps", [P, C])
        rstd = sb("rstd", [P, C])
        half = sb("half", [P, C])
        xn = sb("xn", [P, C, D])
        xnT = sb("xnT", [P, N])
        msgT = sb("msgT", [P, N])
        qT = sb("qT", [P, G, N])
        kT = sb("kT", [P, G, N])
        qTm = sb("qTm", [P, G, N])
        v = sb("v", [P, C, G * P])
        junk = sb("junk", [P, 2, N], BF16)
        maxima = sb("maxima", [P, G, C, P])
        pT = sb("pT", [P, 2, HG, N])
        oT = sb("oT", [P, N])
        den = sb("den", [P, G, C, HG])
        rden = sb("rden", [P, G, C, HG])
        on = sb("on", [P, C, D])
        onT = sb("onT", [P, N])
        x_bo = sb("x_bo", [P, C, D])
        x2 = sb("x2", [P, C, D])
        x2_bo = sb("x2_bo", [P, C, D])
        z = sb("z", [P, C, D])
        zT = sb("zT", [P, N])
        route_t = sb("route_t", [P, C], I32)
        route_r = sb("route_r", [P, GR], I32)
        key_r = sb("key_r", [P, GR])
        key_t = sb("key_t", [P, C])
        less = sb("less", [P, C + 1, GR])
        slot_g = sb("slot_g", [P, C])
        slot = sb("slot", [P, C])
        count = sb("count", [P, 1])
        first = sb("first", [P, 1])
        past = sb("past", [P, N])
        pair_r = sb("pair_r", [P, KH, N])
        onehot = sb("onehot", [P, N])
        turn = sb("turn", [1, 3, PAIRS])
        table = sb("table", [1, 2, PAIRS], I32)
        slot_d = sb("slot_d", [P, C, P])
        slot_r = sb("slot_r", [P, N])
        wsi = sb("wsi", [P, L, KH, HID])
        br_s = sb("br_s", [E, L * HID])
        bs_s = sb("bs_s", [E, L * HID])
        bias = sb("bias", [E, L * HID])
        w = [sb(f"w{l}", [P, E * KH * HID]) for l in range(L)]
        hT = [sb(f"hT{l}", [P, KH, N]) for l in range(L + 1)]
        hs = pT[:, 0, :, :].rearrange("p j (l h) -> p l j h", l=L)
        picked = pT[:, 1, 2:4, :].rearrange("p j n -> p (j n)")[:, 0:3 * KH * P].rearrange(
            "p (b k s) -> p b k s", b=3, k=KH)
        y = pT[:, 1, 0, :].rearrange("p (c d) -> p c d", c=C)
        res = pT[:, 1, 1, :]
        ps = ctx.enter_context(nc.psum_tensor("ps", [P, 8, N], F32))

        def e_(name):
            a, b = EARLY[name]
            return ea[:, a:b]

        def l_(name):
            a, b = LATE[name]
            return la[:, a:b]

        ident = e_("ident")
        wq = e_("wq").rearrange("p (g m) -> p g m", g=G)
        wk = e_("wk").rearrange("p (g m) -> p g m", g=G)
        ws = l_("ws").rearrange("p (l k h) -> p l k h", l=L, k=KH)
        fwo = l_("fwo").rearrange("p (k d) -> p k d", k=KH)
        wi = l_("wi")

        x_in = sem("x_in")
        early_in = sem("early_in")
        adj_in = sem("adj_in")
        adjT_in = sem("adjT_in")
        late_in = sem("late_in")
        route_in = sem("route_in")
        bias_in = sem("bias_in")
        w_in = [sem(f"w{l}_in") for l in range(L)]
        out_done = sem("out_done")
        dve_step = sem("dve_step")
        pool_step = sem("pool_step")
        var_ready = sem("var_ready")
        rstd_ready = sem("rstd_ready")
        half_ready = sem("half_ready")
        xn_ready = sem("xn_ready")
        xnT_psum = sem("xnT_psum")
        xnT_ready = sem("xnT_ready")
        msgT_ready = sem("msgT_ready")
        k_psum = sem("k_psum")
        k_ready = sem("k_ready")
        v_psum = sem("v_psum")
        v_ready = sem("v_ready")
        q_psum = sem("q_psum")
        q_ready = sem("q_ready")
        mask_ready = sem("mask_ready")
        maskT_ready = sem("maskT_ready")
        ident_b_ready = sem("ident_b_ready")
        maxima_zero = sem("maxima_zero")
        max_psum = sem("max_psum")
        max_read = sem("max_read")
        exp_psum = sem("exp_psum")
        exp_ready = sem("exp_ready")
        pv_done = sem("pv_done")
        oT_ready = sem("oT_ready")
        o_psum = sem("o_psum")
        on_ready = sem("on_ready")
        onT_psum = sem("onT_psum")
        onT_ready = sem("onT_ready")
        attn_psum = sem("attn_psum")
        x_bo_ready = sem("x_bo_ready")
        x2_ready = sem("x2_ready")
        x2_bo_ready = sem("x2_bo_ready")
        z_ready = sem("z_ready")
        slot_ready = sem("slot_ready")
        past_ready = sem("past_ready")
        pair_psum = sem("pair_psum")
        pair_ready = sem("pair_ready")
        table_ready = sem("table_ready")
        onehot_ready = sem("onehot_ready")
        gather_ready = sem("gather_ready")
        slot_d_ready = sem("slot_d_ready")
        slot_r_psum = sem("slot_r_psum")
        slot_r_ready = sem("slot_r_ready")
        scatter_ready = sem("scatter_ready")
        wsi_ready = sem("wsi_ready")
        bias_ready = sem("bias_ready")
        zT_psum = sem("zT_psum")
        zT_ready = sem("zT_ready")
        h0_psum = sem("h0_psum")
        h0_act = sem("h0_act")
        h0_dve = sem("h0_dve")
        picked_ready = sem("picked_ready")
        pair_done = sem("pair_done")
        h_ready = sem("h_ready")
        h_turned = sem("h_turned")
        hT_ready = sem("hT_ready")
        y_psum = sem("y_psum")
        y_ready = sem("y_ready")
        out_psum = sem("out_psum")
        res_ready = sem("res_ready")

        block = ctx.enter_context(nc.Block())

        @block.sync
        def _(sp):
            sp.dma_start(xs[:], x.rearrange("(c p) d -> p c d", p=P)).then_inc(x_in, 16)
            sp.dma_start(ea[:], early).then_inc(early_in, 16)
            sp.dma_start(adj_i, adj.rearrange("(c p) n -> p c n", p=P)).then_inc(adj_in, 16)
            sp.dma_start(adjT_i, adjT.rearrange("(c p) n -> p c n", p=P)).then_inc(adjT_in, 16)
            sp.dma_start(route_t[:], route_tok).then_inc(route_in, 16)
            sp.dma_start(route_r[:], route_row.to_broadcast([P, GR])).then_inc(route_in, 16)
            sp.dma_start(la[:], late).then_inc(late_in, 16)
            sp.dma_start(br_s[:], br).then_inc(bias_in, 16)
            sp.dma_start(bs_s[:], bs.to_broadcast([E, L * HID])).then_inc(bias_in, 16)
            part = E // WPARTS * KH * HID
            for l in range(L):
                for n in range(WPARTS):
                    sp.dma_start(w[l][:, n * part:(n + 1) * part],
                                 wr[l, :, n * part:(n + 1) * part]).then_inc(w_in[l], 16)
            sp.wait_ge(res_ready, 1)
            sp.dma_start(out.rearrange("(c p) d -> p c d", p=P), res.rearrange("p (c d) -> p c d", c=C)).then_inc(out_done, 16)
            sp.wait_ge(out_done, 16)

        @block.gpsimd
        def _(pool):
            steps = [0]

            def link(ins):
                steps[0] += 1
                ins.then_inc(pool_step, 1)
                pool.wait_ge(pool_step, steps[0])

            nc.gpsimd.memset(maxima[:], 0.0).then_inc(maxima_zero, 1)
            link(nc.gpsimd.memset(half[:], -0.5))
            pool.wait_ge(var_ready, 1)
            nc.gpsimd.tensor_tensor(rstd[:], var_eps[:], half[:], ALU.pow).then_inc(rstd_ready, 1)
            pool.wait_ge(early_in, 16)
            nc.gpsimd.tensor_copy(ident_b[:], ident).then_inc(ident_b_ready, 1)
            pool.wait_ge(adjT_in, 16)
            for a in range(C):
                nc.gpsimd.tensor_scalar(maskT[:, a, :], adjT_i[:, a, :], 0.0, NEG,
                                        ALU.is_equal, ALU.mult).then_inc(maskT_ready, 1)
            pool.wait_ge(late_in, 16)
            pool.wait_ge(x_in, 16)
            for c in range(C):
                ins = nc.gpsimd.tensor_tensor(x_bo[:, c, :], xs[:, c, :], l_("bo"), ALU.add)
            ins.then_inc(x_bo_ready, 1)
            for l in range(L):
                for k in range(KH):
                    for m in range(KH):
                        cols = slice(m * P, (m + 1) * P)
                        if m == k:
                            ins = nc.gpsimd.tensor_tensor(wsi[:, l, k, cols], ws[:, l, k, cols], ident, ALU.add)
                        else:
                            ins = nc.gpsimd.tensor_copy(wsi[:, l, k, cols], ws[:, l, k, cols])
            ins.then_inc(wsi_ready, 1)
            pool.wait_ge(bias_in, 32)
            nc.gpsimd.tensor_tensor(bias[:], br_s[:], bs_s[:], ALU.add).then_inc(bias_ready, 1)
            pool.wait_ge(slot_ready, 1)
            for c in range(C):
                ins = nc.gpsimd.tensor_scalar(slot_d[:, c, :], ident, slot[:, c:c + 1], None, ALU.mult)
            ins.then_inc(slot_d_ready, 1)
            for c in range(C):
                ins = nc.gpsimd.tensor_scalar(gather[:, c, :], l_("iota"), slot[:, c:c + 1], None, ALU.is_equal)
            ins.then_inc(gather_ready, 1)
            pool.wait_ge(slot_r_ready, 1)
            for c in range(C):
                a = LATE["row_no"][0] + c
                ins = nc.gpsimd.tensor_scalar(scatter[:, c, :], slot_r[:], la[:, a:a + 1], None, ALU.is_equal)
            ins.then_inc(scatter_ready, 1)
            pool.wait_ge(var_ready, 2)
            nc.gpsimd.tensor_tensor(rstd[:], var_eps[:], half[:], ALU.pow).then_inc(rstd_ready, 1)
            pool.wait_ge(x2_ready, 1)
            for c in range(C):
                ins = nc.gpsimd.tensor_tensor(x2_bo[:, c, :], x2[:, c, :], l_("fbo"), ALU.add)
            ins.then_inc(x2_bo_ready, 1)

        @block.scalar
        def _(act):
            act.wait_ge(early_in, 16)
            for g in range(G):
                act.wait_ge(k_psum, g + 1)
                nc.scalar.activation(kT[:, g, :], ps[:, 1 + g, :], ACT.Identity,
                                     bias=e_("bk")[:, g:g + 1]).then_inc(k_ready, 1)
            act.wait_ge(xnT_psum, 1)
            nc.scalar.activation(xnT[:], ps[:, 0, :], ACT.Identity).then_inc(xnT_ready, 1)

            for g in range(G):
                for a in range(C):
                    step = g * C + a
                    if step >= 2:
                        act.wait_ge(pv_done, step - 1)
                    for half_ in range(2):
                        j = 2 * half_
                        act.wait_ge(exp_psum, HG * step + j + 2)
                        nc.scalar.activation(pT[:, step % 2, j:j + 2, :], ps[:, EXPBANK + j:EXPBANK + j + 2, :],
                                             ACT.Exp).then_inc(exp_ready, 1)
                    if g == 1 and a == 0:
                        act.wait_ge(pv_done, C)
                        nc.scalar.activation(oT[:], ps[:, OUTBANK, :], ACT.Identity).then_inc(oT_ready, 1)
                    if g == 1 and a == 1:
                        act.wait_ge(pair_psum, 1)
                        for k in range(KH):
                            ins = nc.scalar.activation(pair_r[:, k, :], ps[:, 1, :], ACT.Identity)
                        ins.then_inc(pair_ready, 1)
                    if g == 1 and a == 2:
                        act.wait_ge(slot_r_psum, 1)
                        nc.scalar.activation(slot_r[:], ps[:, 2, :], ACT.Identity).then_inc(slot_r_ready, 1)
            act.wait_ge(pv_done, G * C)
            act.wait_ge(o_psum, 1)
            nc.scalar.activation(oT[:], ps[:, OUTBANK, :], ACT.Identity).then_inc(oT_ready, 1)
            act.wait_ge(onT_psum, 1)
            nc.scalar.activation(onT[:], ps[:, 0, :], ACT.Identity).then_inc(onT_ready, 1)
            act.wait_ge(zT_psum, 1)
            nc.scalar.activation(zT[:], ps[:, 2, :], ACT.Identity).then_inc(zT_ready, 1)
            act.wait_ge(h0_psum, 1)
            nc.scalar.activation(hT[0][:, 0, :], ps[:, 3, :], ACT.Relu, bias=l_("bi")[:, 0:1]).then_inc(h0_act, 1)
            for l in range(L):
                base = 4 if l == 0 else 0
                for t in range(C):
                    act.wait_ge(pair_done, l * PAIRS + LAST + t)
                    nc.scalar.activation(hs[:, l, t, :], ps[:, base + t, 0:HID], ACT.Relu).then_inc(h_ready, 1)
            for t in range(C):
                act.wait_ge(y_psum, t + 1)
                nc.scalar.activation(y[:, t, :], ps[:, 4 + t, 0:D], ACT.Identity).then_inc(y_ready, 1)

        @block.vector
        def _(dve):
            steps = [0]

            def link(ins):
                steps[0] += 1
                ins.then_inc(dve_step, 1)
                dve.wait_ge(dve_step, steps[0])

            def layernorm(src, dst, n):
                for c in range(C):
                    ins = nc.vector.bn_stats(stats[:, c, :], src[:, c, :])
                link(ins)
                for c in range(C):
                    ins = nc.vector.bn_aggr(mv[:, c, :], stats[:, c, :])
                link(ins)
                nc.vector.tensor_scalar(var_eps[:], mv[:, :, 1], EPS, None, ALU.add).then_inc(var_ready, 1)
                dve.wait_ge(rstd_ready, n)
                for c in range(C):
                    ins = nc.vector.tensor_scalar(dst[:, c, :], src[:, c, :], mv[:, c, 0:1], rstd[:, c:c + 1],
                                                  ALU.subtract, ALU.mult)
                return ins

            dve.wait_ge(early_in, 16)
            a = EARLY["ET"][0] + 1
            nc.vector.tensor_scalar(msgT[:], e_("hnT"), ea[:, a:a + 1], None, ALU.add).then_inc(msgT_ready, 1)
            dve.wait_ge(x_in, 16)
            layernorm(xs, xn, 1).then_inc(xn_ready, 1)
            for g in range(G):
                dve.wait_ge(q_psum, g + 1)
                nc.vector.tensor_scalar(qT[:, g, :], ps[:, 5 + g, :], e_("bq")[:, g:g + 1], DH ** -0.5,
                                        ALU.add, ALU.mult).then_inc(q_ready, 1)
            dve.wait_ge(adj_in, 16)
            link(nc.vector.tensor_scalar(mask[:], adj_i, 0.0, NEG, ALU.is_equal, ALU.mult))
            dve.wait_ge(v_psum, 1)
            for b in range(2):
                ins = nc.vector.tensor_tensor(v[:, 2 * b:2 * b + 2, :], ps[:, 3 + b, :].rearrange("p (a m) -> p a m", a=2),
                                              e_("bv").unsqueeze(1).to_broadcast([P, 2, G * P]), ALU.add)
            ins.then_inc(v_ready, 1)
            dve.wait_ge(maxima_zero, 1)

            def group_max(g):
                u0 = g * (C * HG + 1)
                for c in range(C):
                    for j in range(HG):
                        u = u0 + c * HG + j
                        dve.wait_ge(max_psum, u + 1)
                        if u >= 2:
                            dve.wait_ge(max_read, u - 1)
                        nc.vector.tensor_tensor_reduce(junk[:, u % 2, :], ps[:, u % MAXBANKS, :], mask[:, c, :],
                                                       1.0, FLOOR, ALU.add, ALU.max,
                                                       maxima[:, g, c, HS * j + DH:HS * j + DH + 1]).then_inc(max_read, 1)
                u = u0 + C * HG
                dve.wait_ge(max_psum, u + 1)
                nc.vector.tensor_tensor(qTm[:, g, :], ps[:, u % MAXBANKS, :], qT[:, g, :], ALU.add)\
                    .then_inc(max_read, 1)

            def routing():
                dve.wait_ge(route_in, 32)
                dve.wait_ge(late_in, 16)
                nc.vector.scalar_tensor_tensor(key_r[:], route_r[:], float(GR), l_("iota")[:, 0:GR],
                                               ALU.mult, ALU.add)
                link(nc.vector.scalar_tensor_tensor(key_t[:], route_t[:], float(GR), l_("group_of"),
                                                    ALU.mult, ALU.add))
                for c in range(C):
                    ins = nc.vector.tensor_scalar(less[:, c, :], key_r[:], key_t[:, c:c + 1], None,
                                                  ALU.is_lt, ALU.add, accum_out=slot_g[:, c:c + 1])
                link(ins)
                nc.vector.tensor_scalar(slot[:], slot_g[:], float(RPG), l_("in_group"),
                                        ALU.mult, ALU.add).then_inc(slot_ready, 1)
                link(nc.vector.tensor_scalar(less[0:PAIRS, C, :], route_r[0:PAIRS, :], l_("row_no")[0:PAIRS, 0:1], None,
                                             ALU.is_le, ALU.add, accum_out=count[0:PAIRS, :]))
                link(nc.vector.tensor_scalar(first[0:PAIRS, :], count[0:PAIRS, :], float(RPG), l_("cap")[0:PAIRS, :],
                                             ALU.mult, ALU.min))
                nc.vector.tensor_scalar(past[0:PAIRS, :], l_("iota")[0:PAIRS, :], first[0:PAIRS, :], None,
                                        ALU.is_ge).then_inc(past_ready, 1)

            def pair_table():
                dve.wait_ge(pair_ready, 1)
                nc.vector.scalar_tensor_tensor(onehot[0:E, :], pair_r[0:E, 0, :], l_("row_no")[0:E, 0:1],
                                               l_("tile_of")[0:E, :], ALU.subtract, ALU.is_equal)\
                    .then_inc(onehot_ready, 1)
                numbers = l_("iota")[0:1, 0:PAIRS]
                link(nc.vector.tensor_scalar(turn[:, 0, :], numbers, pair_r[0:1, 0, P:P + 1], None, ALU.is_ge))
                link(nc.vector.scalar_tensor_tensor(turn[:, 1, :], numbers, pair_r[0:1, 0, 2 * P:2 * P + 1],
                                                    turn[:, 0, :], ALU.is_ge, ALU.add))
                link(nc.vector.scalar_tensor_tensor(turn[:, 2, :], numbers, pair_r[0:1, 0, 3 * P:3 * P + 1],
                                                    turn[:, 1, :], ALU.is_ge, ALU.add))
                nc.vector.tensor_tensor(table[:, 0, :], numbers, turn[:, 2, :], ALU.subtract).then_inc(table_ready, 1)
                nc.vector.tensor_copy(table[:, 1, :], turn[:, 2, :]).then_inc(table_ready, 1)

            def normalize(g):
                dve.wait_ge(o_psum, g + 1)
                o = ps[:, OUTBANK, :].rearrange("p (c j m) -> p c j m", c=C, j=HG)
                link(nc.vector.tensor_scalar(den[:, g], o[:, :, :, DH], TINY, None, ALU.max))
                link(nc.vector.reciprocal(rden[:, g], den[:, g]))
                on_g = on[:].rearrange("p c (g j d) -> p g c j d", g=G, j=HG)[:, g]
                for c in range(C):
                    ins = nc.vector.tensor_tensor(on_g[:, c], o[:, c, :, 0:DH],
                                                  rden[:, g, c].unsqueeze(2).to_broadcast([P, HG, DH]), ALU.mult)
                ins.then_inc(on_ready, 1)

            group_max(0)
            routing()
            group_max(1)
            normalize(0)
            pair_table()
            normalize(1)
            dve.wait_ge(attn_psum, 1)
            dve.wait_ge(x_bo_ready, 1)
            ins = nc.vector.tensor_tensor(x2[:].rearrange("p c d -> p (c d)"), ps[:, 1, :],
                                          x_bo[:].rearrange("p c d -> p (c d)"), ALU.add)
            ins.then_inc(x2_ready, 1)
            dve.wait_ge(x2_ready, 1)
            layernorm(x2, z, 2).then_inc(z_ready, 1)
            dve.wait_ge(h0_psum, 2)
            nc.vector.tensor_scalar(hT[0][:, 1, :], ps[:, 0, :], l_("bi")[:, 1:2], 0.0,
                                    ALU.add, ALU.max).then_inc(h0_dve, 1)
            dve.wait_ge(h0_act, 1)
            dve.wait_ge(h0_dve, 1)

            def turned(l, t):
                base = 4 if l == 0 else 0
                dve.wait_ge(h_turned, l * C + t + 1)
                nc.vector.tensor_copy(hT[l + 1][:, :, t * P:(t + 1) * P],
                                      ps[:, base + t, HID:2 * HID].rearrange("p (k s) -> p k s", k=KH))\
                    .then_inc(hT_ready, 1)

            dve.wait_ge(table_ready, 2)
            for l in range(L):
                for i in range(PAIRS):
                    n = l * PAIRS + i
                    if l > 0 and i < C:
                        turned(l - 1, i)
                        dve.wait_ge(hT_ready, (l - 1) * C + i + 1)
                    if n >= 3:
                        dve.wait_ge(pair_done, n - 2)
                    t = dve.value_load(table[0:1, 1, i:i + 1], min_val=0, max_val=C - 1)
                    nc.vector.scalar_tensor_tensor(picked[:, n % 3], pair_r[:, :, bass.ds(t * P, P)], float(i),
                                                   hT[l][:, :, bass.ds(t * P, P)], ALU.is_equal, ALU.mult)\
                        .then_inc(picked_ready, 1)
            for t in range(C):
                turned(L - 1, t)
            dve.wait_ge(out_psum, 1)
            dve.wait_ge(x2_bo_ready, 1)
            nc.vector.tensor_tensor(res, ps[:, 0, :],
                                    x2_bo[:].rearrange("p c d -> p (c d)"), ALU.add).then_inc(res_ready, 1)

        @block.tensor
        def _(pe):
            def mm(o, a, b, start=True, stop=True, pos=None):
                return nc.tensor.matmul(o, a, b, start=start, stop=stop, skip_group_check=True, tile_position=pos)

            pe.wait_ge(msgT_ready, 1)
            for g in range(G):
                mm(ps[:, 1 + g, :], wk[:, g, :], msgT[:]).then_inc(k_psum, 1)
            for a in range(C):
                ins = mm(ps[:, 3 + a // 2, (a % 2) * G * P:(a % 2 + 1) * G * P], msgT[:, a * P:(a + 1) * P], e_("wv"))
            ins.then_inc(v_psum, 1)
            pe.wait_ge(xn_ready, 1)
            for c in range(C):
                ins = nc.tensor.transpose(ps[:, 0, c * P:(c + 1) * P], xn[:, c, :], ident)
            ins.then_inc(xnT_psum, 1)
            pe.wait_ge(xnT_ready, 1)
            for g in range(G):
                mm(ps[:, 5 + g, :], wq[:, g, :], xnT[:]).then_inc(q_psum, 1)

            def rows(j):
                return slice(HS * j, HS * (j + 1))

            def score_rows(g, c):
                for j in range(HG):
                    u = g * (C * HG + 1) + c * HG + j
                    if u >= MAXBANKS:
                        pe.wait_ge(max_read, u - MAXBANKS + 1)
                    mm(ps[:, u % MAXBANKS, :], qT[rows(j), g, c * P:(c + 1) * P], kT[rows(j), g, :],
                       pos=(HS * j, 0)).then_inc(max_psum, 1)

            def turn_maxima(g):
                u = g * (C * HG + 1) + C * HG
                pe.wait_ge(max_read, u)
                for c in range(C):
                    ins = nc.tensor.transpose(ps[:, u % MAXBANKS, c * P:(c + 1) * P], maxima[:, g, c, :], ident)
                ins.then_inc(max_psum, 1)

            def score_cols(g, a):
                step = g * C + a
                for j in range(HG):
                    if step >= 1:
                        pe.wait_ge(exp_ready, 2 * (step - 1) + j // 2 + 1)
                    mm(ps[:, EXPBANK + j, :], ident_b[:], maskT[:, a, :], stop=False)
                for j in range(HG):
                    mm(ps[:, EXPBANK + j, :], kT[rows(j), g, a * P:(a + 1) * P], qTm[rows(j), g, :],
                       start=False, pos=(HS * j, 0)).then_inc(exp_psum, 1)

            def add_values(g, a):
                step = g * C + a
                pe.wait_ge(exp_ready, 2 * step + 2)
                if g > 0 and a == 0:
                    pe.wait_ge(on_ready, g)
                for j in range(HG):
                    ins = mm(ps[rows(j), OUTBANK, :], v[:, a, g * P + HS * j:g * P + HS * (j + 1)], pT[:, step % 2, j, :],
                             start=(a == 0), stop=(a == C - 1), pos=(0, HS * j))
                ins.then_inc(pv_done, 1)

            def turn_outputs(g):
                pe.wait_ge(oT_ready, g + 1)
                for c in range(C):
                    ins = nc.tensor.transpose(ps[:, OUTBANK, c * P:(c + 1) * P], oT[:, c * P:(c + 1) * P], ident)
                ins.then_inc(o_psum, 1)

            pe.wait_ge(k_ready, G)
            pe.wait_ge(q_ready, G)
            for c in range(C):
                score_rows(0, c)
            turn_maxima(0)
            pe.wait_ge(max_read, C * HG + 1)
            pe.wait_ge(ident_b_ready, 1)
            pe.wait_ge(v_ready, 1)
            for a in range(C):
                pe.wait_ge(maskT_ready, a + 1)
                score_cols(0, a)
                if a >= 1:
                    add_values(0, a - 1)
                score_rows(1, a)
            add_values(0, C - 1)
            turn_maxima(1)
            pe.wait_ge(max_read, 2 * (C * HG + 1))
            score_cols(1, 0)
            turn_outputs(0)
            pe.wait_ge(past_ready, 1)
            mm(ps[:, 1, :], l_("ones")[0:PAIRS, :], past[0:PAIRS, :]).then_inc(pair_psum, 1)
            pe.wait_ge(slot_d_ready, 1)
            for c in range(C):
                ins = mm(ps[:, 2, c * P:(c + 1) * P], l_("ones"), slot_d[:, c, :])
            ins.then_inc(slot_r_psum, 1)
            score_cols(1, 1)
            add_values(1, 0)
            score_cols(1, 2)
            add_values(1, 1)
            score_cols(1, 3)
            add_values(1, 2)
            add_values(1, 3)
            turn_outputs(1)
            pe.wait_ge(on_ready, G)
            for c in range(C):
                ins = nc.tensor.transpose(ps[:, 0, c * P:(c + 1) * P], on[:, c, :], ident)
            ins.then_inc(onT_psum, 1)
            pe.wait_ge(onT_ready, 1)
            pe.wait_ge(pair_ready, 1)
            for c in range(C):
                ins = mm(ps[:, 1, c * P:(c + 1) * P], onT[:, c * P:(c + 1) * P], l_("wo"))
            ins.then_inc(attn_psum, 1)

            def acc(l, t):
                return ps[:, (4 if l == 0 else 0) + t, :]

            def add_bias(l):
                for t in range(C):
                    mm(acc(l, t)[:, 0:HID], onehot[0:E, t * P:(t + 1) * P], bias[:, l * HID:(l + 1) * HID], stop=False)

            def add_shared(l, t):
                for k in range(KH):
                    mm(acc(l, t)[:, 0:HID], hT[l][:, k, t * P:(t + 1) * P], wsi[:, l, k, :], start=False, stop=False)

            def turn_window(l, t):
                pe.wait_ge(h_ready, l * C + t + 1)
                for k in range(KH):
                    ins = nc.tensor.transpose(acc(l, t)[:, HID + k * P:HID + (k + 1) * P],
                                              hs[:, l, t, k * P:(k + 1) * P], ident)
                ins.then_inc(h_turned, 1)

            def add_pair(l, i):
                n = l * PAIRS + i
                e = pe.value_load(table[0:1, 0, i:i + 1], min_val=0, max_val=E - 1)
                t = pe.value_load(table[0:1, 1, i:i + 1], min_val=0, max_val=C - 1)
                pe.wait_ge(picked_ready, n + 1)
                flat = ps[:, 4 * (1 - l):4 * (2 - l), :].rearrange("p b n -> p (b n)")
                for k in range(KH):
                    ins = mm(flat[:, bass.ds(t * N, HID)], picked[:, n % 3, k, :],
                             w[l][:, bass.ds(e * (KH * HID) + k * HID, HID)], start=False, stop=(k == KH - 1))
                ins.then_inc(pair_done, 1)

            pe.wait_ge(onehot_ready, 1)
            pe.wait_ge(bias_ready, 1)
            add_bias(0)
            pe.wait_ge(z_ready, 1)
            pe.wait_ge(gather_ready, 1)
            pe.wait_ge(slot_r_ready, 1)
            for c in range(C):
                ins = mm(ps[:, 2, :], z[:, c, :], gather[:, c, :], start=(c == 0), stop=(c == C - 1))
            ins.then_inc(zT_psum, 1)
            pe.wait_ge(zT_ready, 1)
            mm(ps[:, 3, :], wi[:, 0:P], zT[:]).then_inc(h0_psum, 1)
            mm(ps[:, 0, :], wi[:, P:2 * P], zT[:]).then_inc(h0_psum, 1)
            pe.wait_ge(h0_act, 1)
            pe.wait_ge(h0_dve, 1)
            pe.wait_ge(wsi_ready, 1)
            pe.wait_ge(table_ready, 2)
            for t in range(C):
                add_shared(0, t)
            add_bias(1)
            for l in range(L):
                pe.wait_ge(w_in[l], 16 * WPARTS)
                for i in range(PAIRS):
                    add_pair(l, i)
                    if i >= LAST:
                        turn_window(l, i - LAST)
                if l + 1 < L:
                    pe.wait_ge(hT_ready, l * C + 1)
                    add_shared(l + 1, 0)
                turn_window(l, C - 1)
                if l + 1 < L:
                    for t in range(1, C):
                        pe.wait_ge(hT_ready, l * C + t + 1)
                        add_shared(l + 1, t)
            def out_window(t):
                pe.wait_ge(hT_ready, (L - 1) * C + t + 1)
                for k in range(KH):
                    ins = mm(ps[:, 4 + t, 0:D], hT[L][:, k, t * P:(t + 1) * P], fwo[:, k, :], start=(k == 0), stop=(k == KH - 1))
                ins.then_inc(y_psum, 1)

            for t in range(C):
                out_window(t)
            pe.wait_ge(scatter_ready, 1)
            for t in range(C):
                pe.wait_ge(y_ready, t + 1)
                for c in range(C):
                    ins = mm(ps[:, 0, c * P:(c + 1) * P], scatter[:, t, c * P:(c + 1) * P], y[:, t, :],
                             start=(t == 0 and c == 0), stop=(t == C - 1))
            ins.then_inc(out_psum, 1)


def _pack(table, width, parts):
    packed = np.zeros((P, width), np.float32)
    for name, a in parts.items():
        lo, hi = table[name]
        packed[:, lo:hi] = a
    return packed


def _head_columns(a):
    wide = np.zeros((a.shape[0], G * HG, HS), a.dtype)
    wide[:, :, :DH] = a.reshape(a.shape[0], G * HG, DH)
    return wide.reshape(a.shape[0], G * P)


def _head_bias(b, at_maximum):
    wide = np.zeros((G * HG, HS), b.dtype)
    wide[:, :DH] = b.reshape(G * HG, DH)
    wide[:, DH] = at_maximum
    return wide.reshape(G * P)


def kernel(x, adj, L0_gnn_h_neigh, L0_gnn_Wq, L0_gnn_bq, L0_gnn_Wk, L0_gnn_bk, L0_gnn_Wv, L0_gnn_bv, L0_gnn_Wo,
           L0_gnn_bo, L0_gnn_E, L0_ffn_route_id, L0_ffn_Wi, L0_ffn_bi, L0_ffn_Wr, L0_ffn_br, L0_ffn_Ws, L0_ffn_bs,
           L0_ffn_Wo, L0_ffn_bo):
    import concourse.bacc as bacc
    from concourse.bass_utils import run_bass_kernel_spmd

    to = np.asarray
    rows = np.arange(P, dtype=np.float32)[:, None]
    cols = np.arange(N, dtype=np.float32)[None, :]
    early = _pack(EARLY, EARLY_W, {
        "ident": np.eye(P, dtype=np.float32),
        "wq": _head_columns(to(L0_gnn_Wq).T), "bq": _head_bias(to(L0_gnn_bq), 0).reshape(G, P).T,
        "hnT": to(L0_gnn_h_neigh).T, "ET": to(L0_gnn_E).T,
        "wk": _head_columns(to(L0_gnn_Wk).T), "bk": _head_bias(to(L0_gnn_bk), -1).reshape(G, P).T,
        "wv": _head_columns(to(L0_gnn_Wv).T), "bv": _head_bias(to(L0_gnn_bv), 1)[None, :],
    })
    late = _pack(LATE, LATE_W, {
        "wo": to(L0_gnn_Wo).T, "bo": to(L0_gnn_bo)[None, :],
        "iota": cols, "tile_of": cols // P, "ones": np.ones((P, P), np.float32),
        "row_no": rows + P * np.arange(C, dtype=np.float32), "in_group": rows % RPG,
        "group_of": rows // RPG + P // RPG * np.arange(C, dtype=np.float32),
        "cap": np.where(rows < E, 2.0 * N, (rows - E + 1) * P),
        "wi": to(L0_ffn_Wi).T, "bi": to(L0_ffn_bi).reshape(KH, P).T,
        "ws": to(L0_ffn_Ws)[:, 0].transpose(2, 0, 1).reshape(KH, P, L, HID).transpose(1, 2, 0, 3).reshape(P, -1),
        "fwo": to(L0_ffn_Wo).T.reshape(KH, P, D).transpose(1, 0, 2).reshape(P, KH * D),
        "fbo": to(L0_ffn_bo)[None, :],
    })
    route = to(L0_ffn_route_id)
    adj = to(adj)
    arrays = {
        "x": to(x), "early": early, "late": late, "adj": adj, "adjT": adj.T,
        "route_tok": np.repeat(route, RPG).reshape(C, P).T, "route_row": route[None, :],
        "br": to(L0_ffn_br).transpose(1, 0, 2).reshape(E, L * HID),
        "bs": to(L0_ffn_bs).reshape(1, L * HID),
        "wr": to(L0_ffn_Wr).transpose(0, 3, 1, 2).reshape(L, KH, P, E, HID).transpose(0, 2, 3, 1, 4).reshape(L, P, -1),
    }
    nc = bacc.Bacc("TRN2", target_bir_lowering=False, num_devices=1)
    given, args = {}, []
    for name, a in arrays.items():
        given[f"in_{name}"] = np.ascontiguousarray(a)
        args.append(nc.dram_tensor(f"in_{name}", a.shape, mybir.dt.from_np(a.dtype), kind="ExternalInput").ap())
    out = nc.dram_tensor("out", (N, D), F32, kind="ExternalOutput").ap()
    gnn_ffn_kernel(nc, *args, out)
    return run_bass_kernel_spmd(nc, [given], core_ids=[0]).results[0]["out"]
```

```python
from contextlib import ExitStack

import numpy as np

import concourse.bass as bass
from concourse import mybir

ALU = mybir.AluOpType
ACT = mybir.ActivationFunctionType
F32 = mybir.dt.float32
BF16 = mybir.dt.bfloat16
I32 = mybir.dt.int32
F32R = mybir.dt.float32r

P = 128
N = 512
D = 128
C = N // P
H = 8
DH = D // H
HS = 32
HG = P // HS
G = H // HG
HID = 256
KH = HID // P
L = 2
E = 16
GR = 64
RPG = N // GR
PAIRS = E + C - 1
LAST = PAIRS - C + 1
EPS = 1e-5
NEG = -1e30
FLOOR = -1e15
TINY = 1e-30
BLOCKS = ((0, 0), (0, 1), (1, 0), (1, 1))
MROW = len(BLOCKS) * DH
SROWS = 96
MAXBANKS = 3
EXPBANK = 3
OUTBANK = 7
WPARTS = 4

EARLY = {}
LATE = {}


def _columns(table, fields):
    at = 0
    for name, width in fields:
        table[name] = (at, at + width)
        at += width
    return at


EARLY_W = _columns(EARLY, [("ident", P), ("wq", D), ("bq", 1), ("hnT", N), ("ET", 2),
                           ("wk", D), ("bk", 1), ("wv", G * P), ("bv", G * P)])
LATE_W = _columns(LATE, [("wo", D), ("bo", D), ("iota", N), ("tile_of", N), ("ones", P), ("row_no", C),
                         ("group_of", C), ("in_group", 1), ("cap", 1), ("wi", HID), ("bi", KH),
                         ("ws", L * KH * HID), ("fwo", KH * D), ("fbo", D)])


def gnn_ffn_kernel(nc, x, early, late, adj, adjT, route_tok, route_row, br, bs, wr, out):
    with ExitStack() as ctx:
        def sb(name, shape, dt=F32):
            return ctx.enter_context(nc.sbuf_tensor(name, shape, dt))

        def sem(name):
            return ctx.enter_context(nc.semaphore(name))

        xs = sb("xs", [P, C, D])
        ea = sb("ea", [P, EARLY_W])
        la = sb("la", [P, LATE_W])
        gather = sb("gather", [P, C, N])
        scatter = sb("scatter", [P, C, N])
        adj_i = gather[:].bitcast(I32)
        adjT_i = scatter[:].bitcast(I32)
        mask = sb("mask", [P, C, N], BF16)
        maskT = sb("maskT", [P, C, N], BF16)
        ident_b = sb("ident_b", [P, P], BF16)
        stats = sb("stats", [P, C, 6])
        mv = sb("mv", [P, C, 2])
        var_eps = sb("var_eps", [P, C])
        rstd = sb("rstd", [P, C])
        half = sb("half", [P, C])
        xn = sb("xn", [P, C, D])
        xnT = sb("xnT", [P, N])
        msgT = sb("msgT", [P, N])
        q_part = sb("q_part", [P, 2, N], F32R)
        k_part = sb("k_part", [P, 2, N], F32R)
        m_part = sb("m_part", [HG * C, G, 2, P], F32R)
        v = sb("v", [P, C, G * P])
        junk = sb("junk", [P, 2, N], BF16)
        maxima = sb("maxima", [P, G, HG, C])
        pT = sb("pT", [P, 2, HG, N])
        oT = sb("oT", [P, N])
        den = sb("den", [P, G, C, HG])
        rden = sb("rden", [P, G, C, HG])
        on = sb("on", [P, C, D])
        onT = sb("onT", [P, N])
        x_bo = sb("x_bo", [P, C, D])
        x2 = sb("x2", [P, C, D])
        x2_bo = sb("x2_bo", [P, C, D])
        z = sb("z", [P, C, D])
        zT = sb("zT", [P, N])
        route_t = sb("route_t", [P, C], I32)
        route_r = sb("route_r", [P, GR], I32)
        key_r = sb("key_r", [P, GR])
        key_t = sb("key_t", [P, C])
        less = sb("less", [P, C + 1, GR])
        slot_g = sb("slot_g", [P, C])
        slot = sb("slot", [P, C])
        count = sb("count", [P, 1])
        first = sb("first", [P, 1])
        past = sb("past", [P, N])
        pair_r = sb("pair_r", [P, KH, N])
        onehot = sb("onehot", [P, N])
        turn = sb("turn", [1, 3, PAIRS])
        table = sb("table", [1, 2, PAIRS], I32)
        slot_d = sb("slot_d", [P, C, P])
        slot_r = sb("slot_r", [P, N])
        wsi = sb("wsi", [P, L, KH, HID])
        br_s = sb("br_s", [E, L * HID])
        bs_s = sb("bs_s", [E, L * HID])
        bias = sb("bias", [P, L * HID])
        with nc.sbuf_tensor("q_stack", [P, H, N], F32R) as q_stack, nc.sbuf_tensor("k_stack", [P, H, N], F32R) as k_stack:
            pass
        w = [sb("w1", [P, E * KH * HID])]
        w.insert(0, sb("w0", [P, E * KH * HID]))
        hT = [sb(f"hT{l}", [P, KH, N]) for l in range(L + 1)]
        hs = pT[:, 0, :, :].rearrange("p j (l h) -> p l j h", l=L)
        picked = pT[:, 1, 2:4, :].rearrange("p j n -> p (j n)")[:, 0:3 * KH * P].rearrange(
            "p (b k s) -> p b k s", b=3, k=KH)
        y = pT[:, 1, 0, :].rearrange("p (c d) -> p c d", c=C)
        res = pT[:, 1, 1, :]
        ps = ctx.enter_context(nc.psum_tensor("ps", [P, 8, N], F32))

        def e_(name):
            a, b = EARLY[name]
            return ea[:, a:b]

        def l_(name):
            a, b = LATE[name]
            return la[:, a:b]

        ident = e_("ident")
        ws = l_("ws").rearrange("p (l k h) -> p l k h", l=L, k=KH)
        fwo = l_("fwo").rearrange("p (k d) -> p k d", k=KH)
        wi = l_("wi")

        x_in = sem("x_in")
        early_in = sem("early_in")
        adj_in = sem("adj_in")
        adjT_in = sem("adjT_in")
        late_in = sem("late_in")
        route_in = sem("route_in")
        bias_in = sem("bias_in")
        w_in = [sem(f"w{l}_in") for l in range(L)]
        out_done = sem("out_done")
        dve_step = sem("dve_step")
        pool_step = sem("pool_step")
        var_ready = sem("var_ready")
        rstd_ready = sem("rstd_ready")
        xn_ready = sem("xn_ready")
        xnT_psum = sem("xnT_psum")
        xnT_ready = sem("xnT_ready")
        msgT_ready = sem("msgT_ready")
        k_psum = sem("k_psum")
        v_psum = sem("v_psum")
        v_ready = sem("v_ready")
        q_psum = sem("q_psum")
        mask_ready = sem("mask_ready")
        maskT_ready = sem("maskT_ready")
        ident_b_ready = sem("ident_b_ready")
        stack_rows = sem("stack_rows")
        k_stacked = sem("k_stacked")
        q_stacked = sem("q_stacked")
        m_psum = sem("m_psum")
        m_high = sem("m_high")
        m_low = sem("m_low")
        m_stacked = sem("m_stacked")
        k_high = sem("k_high")
        k_low = sem("k_low")
        q_high = sem("q_high")
        q_low = sem("q_low")
        max_psum = sem("max_psum")
        max_read = sem("max_read")
        exp_psum = sem("exp_psum")
        exp_ready = sem("exp_ready")
        pv_done = sem("pv_done")
        oT_ready = sem("oT_ready")
        o_psum = sem("o_psum")
        on_ready = sem("on_ready")
        onT_psum = sem("onT_psum")
        onT_ready = sem("onT_ready")
        attn_psum = sem("attn_psum")
        x_bo_ready = sem("x_bo_ready")
        x2_ready = sem("x2_ready")
        x2_bo_ready = sem("x2_bo_ready")
        z_ready = sem("z_ready")
        slot_ready = sem("slot_ready")
        past_ready = sem("past_ready")
        pair_psum = sem("pair_psum")
        pair_ready = sem("pair_ready")
        table_ready = sem("table_ready")
        onehot_ready = sem("onehot_ready")
        gather_ready = sem("gather_ready")
        slot_d_ready = sem("slot_d_ready")
        slot_r_psum = sem("slot_r_psum")
        slot_r_ready = sem("slot_r_ready")
        scatter_ready = sem("scatter_ready")
        wsi_ready = sem("wsi_ready")
        bias_ready = sem("bias_ready")
        zT_psum = sem("zT_psum")
        zT_ready = sem("zT_ready")
        h0_psum = sem("h0_psum")
        h0_act = sem("h0_act")
        h0_dve = sem("h0_dve")
        picked_ready = sem("picked_ready")
        pair_done = sem("pair_done")
        h_ready = sem("h_ready")
        h_turned = sem("h_turned")
        hT_ready = sem("hT_ready")
        y_psum = sem("y_psum")
        y_ready = sem("y_ready")
        out_psum = sem("out_psum")
        res_ready = sem("res_ready")

        block = ctx.enter_context(nc.Block())

        @block.sync
        def _(sp):
            sp.dma_start(xs[:], x.rearrange("(c p) d -> p c d", p=P)).then_inc(x_in, 16)
            sp.dma_start(ea[:], early).then_inc(early_in, 16)
            sp.dma_start(adj_i, adj.rearrange("(c p) n -> p c n", p=P)).then_inc(adj_in, 16)
            sp.dma_start(adjT_i, adjT.rearrange("(c p) n -> p c n", p=P)).then_inc(adjT_in, 16)
            sp.dma_start(route_t[:], route_tok).then_inc(route_in, 16)
            sp.dma_start(route_r[:], route_row.to_broadcast([P, GR])).then_inc(route_in, 16)
            sp.dma_start(la[:], late).then_inc(late_in, 16)
            sp.dma_start(br_s[:], br).then_inc(bias_in, 16)
            sp.dma_start(bs_s[:], bs.to_broadcast([E, L * HID])).then_inc(bias_in, 16)
            part = E // WPARTS * KH * HID

            def load_weights(l, n):
                sp.dma_start(w[l][:, n * part:(n + 1) * part], wr[l, :, n * part:(n + 1) * part]).then_inc(w_in[l], 16)

            def stack(dst, src, side, signal):
                for n, parts in enumerate(BLOCKS):
                    sp.dma_start(dst[n * DH:(n + 1) * DH, :, :].bitcast(F32),
                                 src[:, parts[side], :].bitcast(F32)).then_inc(signal, 16)

            load_weights(0, 0)
            sp.wait_ge(k_high, 1)
            sp.wait_ge(k_low, 1)
            stack(k_stack, k_part, 1, k_stacked)
            sp.wait_ge(q_high, 1)
            sp.wait_ge(q_low, 1)
            stack(q_stack, q_part, 0, q_stacked)
            load_weights(0, 1)
            load_weights(0, 2)
            for g in range(G):
                sp.wait_ge(m_high, g + 1)
                sp.wait_ge(m_low, g + 1)
                for n in range(2):
                    sp.dma_start(q_stack[MROW + n:MROW + n + 1, g * HG:(g + 1) * HG, :].bitcast(F32),
                                 m_part[:, g, n, :].bitcast(F32)).then_inc(m_stacked, 16)
                if g == 0:
                    load_weights(0, 3)
            sp.wait_ge(exp_psum, G * C * 2)
            for n in range(WPARTS):
                load_weights(1, n)
            sp.wait_ge(res_ready, 1)
            sp.dma_start(out.rearrange("(c p) d -> p c d", p=P), res.rearrange("p (c d) -> p c d", c=C)).then_inc(out_done, 16)
            sp.wait_ge(out_done, 16)

        @block.gpsimd
        def _(pool):
            steps = [0]

            def link(ins):
                steps[0] += 1
                ins.then_inc(pool_step, 1)
                pool.wait_ge(pool_step, steps[0])

            link(nc.gpsimd.memset(half[:], -0.5))
            nc.gpsimd.memset(q_stack[MROW:SROWS, :, :].bitcast(F32), 0.0).then_inc(stack_rows, 1)
            pool.wait_ge(stack_rows, 1)
            pool.wait_ge(var_ready, 1)
            nc.gpsimd.tensor_tensor(rstd[:], var_eps[:], half[:], ALU.pow).then_inc(rstd_ready, 1)
            pool.wait_ge(rstd_ready, 1)
            nc.gpsimd.memset(k_stack[MROW:SROWS, :, :].bitcast(F32), -1.0).then_inc(stack_rows, 1)
            pool.wait_ge(stack_rows, 2)
            pool.wait_ge(early_in, 16)
            nc.gpsimd.tensor_copy(ident_b[:], ident).then_inc(ident_b_ready, 1)
            pool.wait_ge(adjT_in, 16)
            for a in range(C):
                nc.gpsimd.tensor_scalar(maskT[:, a, :], adjT_i[:, a, :], 0.0, NEG,
                                        ALU.is_equal, ALU.mult).then_inc(maskT_ready, 1)
            pool.wait_ge(late_in, 16)
            pool.wait_ge(x_in, 16)
            for c in range(C):
                ins = nc.gpsimd.tensor_tensor(x_bo[:, c, :], xs[:, c, :], l_("bo"), ALU.add)
            ins.then_inc(x_bo_ready, 1)
            for l in range(L):
                for k in range(KH):
                    for m in range(KH):
                        cols = slice(m * P, (m + 1) * P)
                        if m == k:
                            ins = nc.gpsimd.tensor_tensor(wsi[:, l, k, cols], ws[:, l, k, cols], ident, ALU.add)
                        else:
                            ins = nc.gpsimd.tensor_copy(wsi[:, l, k, cols], ws[:, l, k, cols])
            ins.then_inc(wsi_ready, 1)
            pool.wait_ge(bias_in, 32)
            link(nc.gpsimd.memset(bias[:], 0.0))
            nc.gpsimd.tensor_tensor(bias[0:E, :], br_s[:], bs_s[:], ALU.add).then_inc(bias_ready, 1)
            pool.wait_ge(bias_ready, 1)
            pool.wait_ge(slot_ready, 1)
            for c in range(C):
                ins = nc.gpsimd.tensor_scalar(slot_d[:, c, :], ident, slot[:, c:c + 1], None, ALU.mult)
            ins.then_inc(slot_d_ready, 1)
            for c in range(C):
                ins = nc.gpsimd.tensor_scalar(gather[:, c, :], l_("iota"), slot[:, c:c + 1], None, ALU.is_equal)
            ins.then_inc(gather_ready, 1)
            pool.wait_ge(slot_r_ready, 1)
            for c in range(C):
                a = LATE["row_no"][0] + c
                ins = nc.gpsimd.tensor_scalar(scatter[:, c, :], slot_r[:], la[:, a:a + 1], None, ALU.is_equal)
            ins.then_inc(scatter_ready, 1)
            pool.wait_ge(var_ready, 2)
            nc.gpsimd.tensor_tensor(rstd[:], var_eps[:], half[:], ALU.pow).then_inc(rstd_ready, 1)
            pool.wait_ge(x2_ready, 1)
            for c in range(C):
                ins = nc.gpsimd.tensor_tensor(x2_bo[:, c, :], x2[:, c, :], l_("fbo"), ALU.add)
            ins.then_inc(x2_bo_ready, 1)

        @block.scalar
        def _(act):
            act.wait_ge(early_in, 16)
            act.wait_ge(k_psum, 1)
            nc.scalar.activation(k_part[:, 0, :], ps[:, 1, :], ACT.Identity, bias=e_("bk")).then_inc(k_high, 1)
            act.wait_ge(xnT_psum, 1)
            nc.scalar.activation(xnT[:], ps[:, 0, :], ACT.Identity).then_inc(xnT_ready, 1)
            act.wait_ge(q_psum, 1)
            nc.scalar.activation(q_part[:, 0, :], ps[:, 2, :], ACT.Identity, bias=e_("bq")).then_inc(q_high, 1)

            def maxima_high(g):
                act.wait_ge(m_psum, g + 1)
                u = g * (C * HG + 1) + C * HG
                nc.scalar.activation(m_part[:, g, 0, :], ps[0:HG * C, u % MAXBANKS, 0:P], ACT.Identity)\
                    .then_inc(m_high, 1)

            maxima_high(0)
            for g in range(G):
                for a in range(C):
                    step = g * C + a
                    if step >= 2:
                        act.wait_ge(pv_done, step - 1)
                    for half_ in range(2):
                        j = 2 * half_
                        act.wait_ge(exp_psum, 2 * step + half_ + 1)
                        nc.scalar.activation(pT[:, step % 2, j:j + 2, :], ps[:, EXPBANK + j:EXPBANK + j + 2, :],
                                             ACT.Exp, scale=DH ** -0.5).then_inc(exp_ready, 1)
                    if g == 0 and a == C - 1:
                        maxima_high(1)
                    if g == 1 and a == 0:
                        act.wait_ge(pv_done, C)
                        nc.scalar.activation(oT[:], ps[:, OUTBANK, :], ACT.Identity).then_inc(oT_ready, 1)
                    if g == 1 and a == 1:
                        act.wait_ge(pair_psum, 1)
                        for k in range(KH):
                            ins = nc.scalar.activation(pair_r[:, k, :], ps[:, 1, :], ACT.Identity)
                        ins.then_inc(pair_ready, 1)
                    if g == 1 and a == 2:
                        act.wait_ge(slot_r_psum, 1)
                        nc.scalar.activation(slot_r[:], ps[:, 2, :], ACT.Identity).then_inc(slot_r_ready, 1)
            act.wait_ge(pv_done, G * C)
            act.wait_ge(o_psum, 1)
            nc.scalar.activation(oT[:], ps[:, OUTBANK, :], ACT.Identity).then_inc(oT_ready, 1)
            act.wait_ge(onT_psum, 1)
            nc.scalar.activation(onT[:], ps[:, 0, :], ACT.Identity).then_inc(onT_ready, 1)
            act.wait_ge(zT_psum, 1)
            nc.scalar.activation(zT[:], ps[:, 2, :], ACT.Identity).then_inc(zT_ready, 1)
            act.wait_ge(h0_psum, 1)
            nc.scalar.activation(hT[0][:, 0, :], ps[:, 3, :], ACT.Relu, bias=l_("bi")[:, 0:1]).then_inc(h0_act, 1)
            for l in range(L):
                base = 4 if l == 0 else 0
                for t in range(C):
                    act.wait_ge(pair_done, l * PAIRS + LAST + t)
                    nc.scalar.activation(hs[:, l, t, :], ps[:, base + t, 0:HID], ACT.Relu).then_inc(h_ready, 1)
            for t in range(C):
                act.wait_ge(y_psum, t + 1)
                nc.scalar.activation(y[:, t, :], ps[:, 4 + t, 0:D], ACT.Identity).then_inc(y_ready, 1)

        @block.vector
        def _(dve):
            steps = [0]

            def link(ins):
                steps[0] += 1
                ins.then_inc(dve_step, 1)
                dve.wait_ge(dve_step, steps[0])

            def layernorm(src, dst, n):
                for c in range(C):
                    ins = nc.vector.bn_stats(stats[:, c, :], src[:, c, :])
                link(ins)
                for c in range(C):
                    ins = nc.vector.bn_aggr(mv[:, c, :], stats[:, c, :])
                link(ins)
                nc.vector.tensor_scalar(var_eps[:], mv[:, :, 1], EPS, None, ALU.add).then_inc(var_ready, 1)
                dve.wait_ge(rstd_ready, n)
                for c in range(C):
                    ins = nc.vector.tensor_scalar(dst[:, c, :], src[:, c, :], mv[:, c, 0:1], rstd[:, c:c + 1],
                                                  ALU.subtract, ALU.mult)
                return ins

            dve.wait_ge(early_in, 16)
            a = EARLY["ET"][0] + 1
            nc.vector.tensor_scalar(msgT[:], e_("hnT"), ea[:, a:a + 1], None, ALU.add).then_inc(msgT_ready, 1)
            dve.wait_ge(x_in, 16)
            layernorm(xs, xn, 1).then_inc(xn_ready, 1)

            def low_part(bank, bias_, part, signal):
                nc.vector.scalar_tensor_tensor(part[:, 1, :], ps[:, bank, :], bias_, part[:, 0, :].bitcast(F32),
                                               ALU.add, ALU.subtract).then_inc(signal, 1)

            dve.wait_ge(k_high, 1)
            low_part(1, e_("bk"), k_part, k_low)
            dve.wait_ge(q_high, 1)
            low_part(2, e_("bq"), q_part, q_low)
            dve.wait_ge(adj_in, 16)
            link(nc.vector.tensor_scalar(mask[:], adj_i, 0.0, NEG, ALU.is_equal, ALU.mult))
            dve.wait_ge(v_psum, 1)
            for b in range(2):
                ins = nc.vector.tensor_tensor(v[:, 2 * b:2 * b + 2, :], ps[:, 3 + b, :].rearrange("p (a m) -> p a m", a=2),
                                              e_("bv").unsqueeze(1).to_broadcast([P, 2, G * P]), ALU.add)
            ins.then_inc(v_ready, 1)
            def group_max(g):
                u0 = g * (C * HG + 1)
                for c in range(C):
                    for j in range(HG):
                        u = u0 + c * HG + j
                        n = g * C * HG + c * HG + j
                        dve.wait_ge(max_psum, n + 1)
                        if n >= 2:
                            dve.wait_ge(max_read, n - 1)
                        nc.vector.tensor_tensor_reduce(junk[:, n % 2, :], ps[:, u % MAXBANKS, :], mask[:, c, :],
                                                       1.0, FLOOR, ALU.add, ALU.max,
                                                       maxima[:, g, j, c:c + 1]).then_inc(max_read, 1)
                u = u0 + C * HG
                dve.wait_ge(m_high, g + 1)
                nc.vector.tensor_tensor(m_part[:, g, 1, :], ps[0:HG * C, u % MAXBANKS, 0:P],
                                        m_part[:, g, 0, :].bitcast(F32), ALU.subtract).then_inc(m_low, 1)

            def routing():
                dve.wait_ge(route_in, 32)
                dve.wait_ge(late_in, 16)
                nc.vector.scalar_tensor_tensor(key_r[:], route_r[:], float(GR), l_("iota")[:, 0:GR],
                                               ALU.mult, ALU.add)
                link(nc.vector.scalar_tensor_tensor(key_t[:], route_t[:], float(GR), l_("group_of"),
                                                    ALU.mult, ALU.add))
                for c in range(C):
                    ins = nc.vector.tensor_scalar(less[:, c, :], key_r[:], key_t[:, c:c + 1], None,
                                                  ALU.is_lt, ALU.add, accum_out=slot_g[:, c:c + 1])
                link(ins)
                nc.vector.tensor_scalar(slot[:], slot_g[:], float(RPG), l_("in_group"),
                                        ALU.mult, ALU.add).then_inc(slot_ready, 1)
                link(nc.vector.tensor_scalar(less[:, C, :], route_r[:, :], l_("row_no")[:, 0:1], None,
                                             ALU.is_le, ALU.add, accum_out=count[:, :]))
                link(nc.vector.tensor_scalar(first[:, :], count[:, :], float(RPG), l_("cap")[:, :],
                                             ALU.mult, ALU.min))
                nc.vector.tensor_scalar(past[:, :], l_("iota")[:, :], first[:, :], None,
                                        ALU.is_ge).then_inc(past_ready, 1)

            def pair_table():
                dve.wait_ge(pair_ready, 1)
                nc.vector.scalar_tensor_tensor(onehot[:], pair_r[:, 0, :], l_("row_no")[:, 0:1],
                                               l_("tile_of"), ALU.subtract, ALU.is_equal)\
                    .then_inc(onehot_ready, 1)
                numbers = l_("iota")[0:1, 0:PAIRS]
                link(nc.vector.tensor_scalar(turn[:, 0, :], numbers, pair_r[0:1, 0, P:P + 1], None, ALU.is_ge))
                link(nc.vector.scalar_tensor_tensor(turn[:, 1, :], numbers, pair_r[0:1, 0, 2 * P:2 * P + 1],
                                                    turn[:, 0, :], ALU.is_ge, ALU.add))
                link(nc.vector.scalar_tensor_tensor(turn[:, 2, :], numbers, pair_r[0:1, 0, 3 * P:3 * P + 1],
                                                    turn[:, 1, :], ALU.is_ge, ALU.add))
                nc.vector.tensor_tensor(table[:, 0, :], numbers, turn[:, 2, :], ALU.subtract).then_inc(table_ready, 1)
                nc.vector.tensor_copy(table[:, 1, :], turn[:, 2, :]).then_inc(table_ready, 1)

            def normalize(g):
                dve.wait_ge(o_psum, g + 1)
                o = ps[:, OUTBANK, :].rearrange("p (c j m) -> p c j m", c=C, j=HG)
                link(nc.vector.tensor_scalar(den[:, g], o[:, :, :, DH], TINY, None, ALU.max))
                link(nc.vector.reciprocal(rden[:, g], den[:, g]))
                on_g = on[:].rearrange("p c (g j d) -> p g c j d", g=G, j=HG)[:, g]
                for c in range(C):
                    ins = nc.vector.tensor_tensor(on_g[:, c], o[:, c, :, 0:DH],
                                                  rden[:, g, c].unsqueeze(2).to_broadcast([P, HG, DH]), ALU.mult)
                ins.then_inc(on_ready, 1)

            group_max(0)
            routing()
            group_max(1)
            normalize(0)
            pair_table()
            normalize(1)
            dve.wait_ge(attn_psum, 1)
            dve.wait_ge(x_bo_ready, 1)
            ins = nc.vector.tensor_tensor(x2[:].rearrange("p c d -> p (c d)"), ps[:, 1, :],
                                          x_bo[:].rearrange("p c d -> p (c d)"), ALU.add)
            ins.then_inc(x2_ready, 1)
            dve.wait_ge(x2_ready, 1)
            layernorm(x2, z, 2).then_inc(z_ready, 1)
            dve.wait_ge(h0_psum, 2)
            nc.vector.tensor_scalar(hT[0][:, 1, :], ps[:, 0, :], l_("bi")[:, 1:2], 0.0,
                                    ALU.add, ALU.max).then_inc(h0_dve, 1)
            dve.wait_ge(h0_act, 1)
            dve.wait_ge(h0_dve, 1)

            def turned(l, t):
                base = 4 if l == 0 else 0
                dve.wait_ge(h_turned, l * C + t + 1)
                nc.vector.tensor_copy(hT[l + 1][:, :, t * P:(t + 1) * P],
                                      ps[:, base + t, HID:2 * HID].rearrange("p (k s) -> p k s", k=KH))\
                    .then_inc(hT_ready, 1)

            dve.wait_ge(table_ready, 2)
            for l in range(L):
                for i in range(PAIRS):
                    n = l * PAIRS + i
                    if l > 0 and i < C:
                        turned(l - 1, i)
                        dve.wait_ge(hT_ready, (l - 1) * C + i + 1)
                    if n >= 3:
                        dve.wait_ge(pair_done, n - 2)
                    t = dve.value_load(table[0:1, 1, i:i + 1], min_val=0, max_val=C - 1)
                    nc.vector.scalar_tensor_tensor(picked[:, n % 3], pair_r[:, :, bass.ds(t * P, P)], float(i),
                                                   hT[l][:, :, bass.ds(t * P, P)], ALU.is_equal, ALU.mult)\
                        .then_inc(picked_ready, 1)
            for t in range(C):
                turned(L - 1, t)
            dve.wait_ge(out_psum, 1)
            dve.wait_ge(x2_bo_ready, 1)
            nc.vector.tensor_tensor(res, ps[:, 0, :],
                                    x2_bo[:].rearrange("p c d -> p (c d)"), ALU.add).then_inc(res_ready, 1)

        @block.tensor
        def _(pe):
            def mm(o, a, b, start=True, stop=True, pos=None):
                return nc.tensor.matmul(o, a, b, start=start, stop=stop, skip_group_check=True, tile_position=pos)

            pe.wait_ge(msgT_ready, 1)
            mm(ps[:, 1, :], e_("wk"), msgT[:]).then_inc(k_psum, 1)
            for a in range(C):
                ins = mm(ps[:, 3 + a // 2, (a % 2) * G * P:(a % 2 + 1) * G * P], msgT[:, a * P:(a + 1) * P], e_("wv"))
            ins.then_inc(v_psum, 1)
            pe.wait_ge(xn_ready, 1)
            for c in range(C):
                ins = nc.tensor.transpose(ps[:, 0, c * P:(c + 1) * P], xn[:, c, :], ident)
            ins.then_inc(xnT_psum, 1)
            pe.wait_ge(xnT_ready, 1)
            mm(ps[:, 2, :], e_("wq"), xnT[:]).then_inc(q_psum, 1)

            def score_rows(g, c):
                for j in range(HG):
                    u = g * (C * HG + 1) + c * HG + j
                    n = g * C * HG + c * HG + j
                    if g > 0 and c * HG + j < MAXBANKS:
                        pe.wait_ge(m_low, g)
                    if n >= MAXBANKS:
                        pe.wait_ge(max_read, n - MAXBANKS + 1)
                    h = g * HG + j
                    mm(ps[:, u % MAXBANKS, :], q_stack[0:SROWS, h, c * P:(c + 1) * P], k_stack[0:SROWS, h, :])\
                        .then_inc(max_psum, 1)

            def turn_maxima(g):
                u = g * (C * HG + 1) + C * HG
                pe.wait_ge(max_read, (g + 1) * C * HG)
                nc.tensor.transpose(ps[0:HG * C, u % MAXBANKS, 0:P], maxima[:, g].rearrange("p j c -> p (j c)"),
                                    ident).then_inc(m_psum, 1)

            def score_cols(g, a):
                step = g * C + a
                for pair in range(2):
                    if step >= 1:
                        pe.wait_ge(exp_ready, 2 * (step - 1) + pair + 1)
                    for j in (2 * pair, 2 * pair + 1):
                        mm(ps[:, EXPBANK + j, :], ident_b[:], maskT[:, a, :], stop=False)
                    for j in (2 * pair, 2 * pair + 1):
                        ins = mm(ps[:, EXPBANK + j, :], k_stack[0:SROWS, g * HG + j, a * P:(a + 1) * P],
                                 q_stack[0:SROWS, g * HG + j, :], start=False)
                    ins.then_inc(exp_psum, 1)

            def add_values(g, a):
                step = g * C + a
                pe.wait_ge(exp_ready, 2 * step + 2)
                if g > 0 and a == 0:
                    pe.wait_ge(on_ready, g)
                for j in range(HG):
                    ins = mm(ps[HS * j:HS * (j + 1), OUTBANK, :], v[:, a, g * P + HS * j:g * P + HS * (j + 1)], pT[:, step % 2, j, :],
                             start=(a == 0), stop=(a == C - 1), pos=(0, HS * j))
                ins.then_inc(pv_done, 1)

            def turn_outputs(g):
                pe.wait_ge(oT_ready, g + 1)
                for c in range(C):
                    ins = nc.tensor.transpose(ps[:, OUTBANK, c * P:(c + 1) * P], oT[:, c * P:(c + 1) * P], ident)
                ins.then_inc(o_psum, 1)

            pe.wait_ge(stack_rows, 2)
            pe.wait_ge(k_stacked, 16 * len(BLOCKS))
            pe.wait_ge(q_stacked, 16 * len(BLOCKS))
            pe.wait_ge(q_low, 1)
            for c in range(C):
                score_rows(0, c)
            turn_maxima(0)
            score_rows(1, 0)
            pe.wait_ge(ident_b_ready, 1)
            pe.wait_ge(v_ready, 1)
            pe.wait_ge(m_stacked, 2 * 16)
            for a in range(C):
                pe.wait_ge(maskT_ready, a + 1)
                score_cols(0, a)
                if a >= 1:
                    add_values(0, a - 1)
                if a + 1 < C:
                    score_rows(1, a + 1)
            add_values(0, C - 1)
            turn_maxima(1)
            pe.wait_ge(m_stacked, 2 * 2 * 16)
            score_cols(1, 0)
            turn_outputs(0)
            pe.wait_ge(past_ready, 1)
            mm(ps[:, 1, :], l_("ones"), past[:]).then_inc(pair_psum, 1)
            pe.wait_ge(slot_d_ready, 1)
            for c in range(C):
                ins = mm(ps[:, 2, c * P:(c + 1) * P], l_("ones"), slot_d[:, c, :])
            ins.then_inc(slot_r_psum, 1)
            score_cols(1, 1)
            add_values(1, 0)
            score_cols(1, 2)
            add_values(1, 1)
            score_cols(1, 3)
            add_values(1, 2)
            add_values(1, 3)
            turn_outputs(1)
            pe.wait_ge(on_ready, G)
            for c in range(C):
                ins = nc.tensor.transpose(ps[:, 0, c * P:(c + 1) * P], on[:, c, :], ident)
            ins.then_inc(onT_psum, 1)
            pe.wait_ge(onT_ready, 1)
            pe.wait_ge(pair_ready, 1)
            for c in range(C):
                ins = mm(ps[:, 1, c * P:(c + 1) * P], onT[:, c * P:(c + 1) * P], l_("wo"))
            ins.then_inc(attn_psum, 1)

            def acc(l, t):
                return ps[:, (4 if l == 0 else 0) + t, :]

            def add_bias(l):
                for t in range(C):
                    mm(acc(l, t)[:, 0:HID], onehot[:, t * P:(t + 1) * P], bias[:, l * HID:(l + 1) * HID], stop=False)

            def add_shared(l, t):
                for k in range(KH):
                    mm(acc(l, t)[:, 0:HID], hT[l][:, k, t * P:(t + 1) * P], wsi[:, l, k, :], start=False, stop=False)

            def turn_window(l, t):
                pe.wait_ge(h_ready, l * C + t + 1)
                for k in range(KH):
                    ins = nc.tensor.transpose(acc(l, t)[:, HID + k * P:HID + (k + 1) * P],
                                              hs[:, l, t, k * P:(k + 1) * P], ident)
                ins.then_inc(h_turned, 1)

            def add_pair(l, i):
                n = l * PAIRS + i
                e = pe.value_load(table[0:1, 0, i:i + 1], min_val=0, max_val=E - 1)
                t = pe.value_load(table[0:1, 1, i:i + 1], min_val=0, max_val=C - 1)
                pe.wait_ge(picked_ready, n + 1)
                flat = ps[:, 4 * (1 - l):4 * (2 - l), :].rearrange("p b n -> p (b n)")
                for k in range(KH):
                    ins = mm(flat[:, bass.ds(t * N, HID)], picked[:, n % 3, k, :],
                             w[l][:, bass.ds(e * (KH * HID) + k * HID, HID)], start=False, stop=(k == KH - 1))
                ins.then_inc(pair_done, 1)

            pe.wait_ge(onehot_ready, 1)
            pe.wait_ge(bias_ready, 1)
            add_bias(0)
            pe.wait_ge(z_ready, 1)
            pe.wait_ge(gather_ready, 1)
            pe.wait_ge(slot_r_ready, 1)
            for c in range(C):
                ins = mm(ps[:, 2, :], z[:, c, :], gather[:, c, :], start=(c == 0), stop=(c == C - 1))
            ins.then_inc(zT_psum, 1)
            pe.wait_ge(zT_ready, 1)
            mm(ps[:, 3, :], wi[:, 0:P], zT[:]).then_inc(h0_psum, 1)
            mm(ps[:, 0, :], wi[:, P:2 * P], zT[:]).then_inc(h0_psum, 1)
            pe.wait_ge(h0_act, 1)
            pe.wait_ge(h0_dve, 1)
            pe.wait_ge(wsi_ready, 1)
            pe.wait_ge(table_ready, 2)
            for t in range(C):
                add_shared(0, t)
            add_bias(1)
            for l in range(L):
                pe.wait_ge(w_in[l], 16 * WPARTS)
                for i in range(PAIRS):
                    add_pair(l, i)
                    if i >= LAST:
                        turn_window(l, i - LAST)
                if l + 1 < L:
                    pe.wait_ge(hT_ready, l * C + 1)
                    add_shared(l + 1, 0)
                turn_window(l, C - 1)
                if l + 1 < L:
                    for t in range(1, C):
                        pe.wait_ge(hT_ready, l * C + t + 1)
                        add_shared(l + 1, t)
            def out_window(t):
                pe.wait_ge(hT_ready, (L - 1) * C + t + 1)
                for k in range(KH):
                    ins = mm(ps[:, 4 + t, 0:D], hT[L][:, k, t * P:(t + 1) * P], fwo[:, k, :], start=(k == 0), stop=(k == KH - 1))
                ins.then_inc(y_psum, 1)

            for t in range(C):
                out_window(t)
            pe.wait_ge(scatter_ready, 1)
            for t in range(C):
                pe.wait_ge(y_ready, t + 1)
                for c in range(C):
                    ins = mm(ps[:, 0, c * P:(c + 1) * P], scatter[:, t, c * P:(c + 1) * P], y[:, t, :],
                             start=(t == 0 and c == 0), stop=(t == C - 1))
            ins.then_inc(out_psum, 1)


def _pack(table, width, parts):
    packed = np.zeros((P, width), np.float32)
    for name, a in parts.items():
        lo, hi = table[name]
        packed[:, lo:hi] = a
    return packed


def _by_d(a):
    return a.reshape(H, DH, *a.shape[1:]).swapaxes(0, 1).reshape(a.shape)


def _head_columns(a):
    wide = np.zeros((a.shape[0], G * HG, HS), a.dtype)
    wide[:, :, :DH] = a.reshape(a.shape[0], G * HG, DH)
    return wide.reshape(a.shape[0], G * P)


def _head_bias(b):
    wide = np.zeros((G * HG, HS), b.dtype)
    wide[:, :DH] = b.reshape(G * HG, DH)
    wide[:, DH] = 1
    return wide.reshape(G * P)


def kernel(x, adj, L0_gnn_h_neigh, L0_gnn_Wq, L0_gnn_bq, L0_gnn_Wk, L0_gnn_bk, L0_gnn_Wv, L0_gnn_bv, L0_gnn_Wo,
           L0_gnn_bo, L0_gnn_E, L0_ffn_route_id, L0_ffn_Wi, L0_ffn_bi, L0_ffn_Wr, L0_ffn_br, L0_ffn_Ws, L0_ffn_bs,
           L0_ffn_Wo, L0_ffn_bo):
    import concourse.bacc as bacc
    from concourse.bass_utils import run_bass_kernel_spmd

    to = np.asarray
    rows = np.arange(P, dtype=np.float32)[:, None]
    cols = np.arange(N, dtype=np.float32)[None, :]
    early = _pack(EARLY, EARLY_W, {
        "ident": np.eye(P, dtype=np.float32),
        "wq": _by_d(to(L0_gnn_Wq)).T, "bq": _by_d(to(L0_gnn_bq))[:, None],
        "hnT": to(L0_gnn_h_neigh).T, "ET": to(L0_gnn_E).T,
        "wk": _by_d(to(L0_gnn_Wk)).T, "bk": _by_d(to(L0_gnn_bk))[:, None],
        "wv": _head_columns(to(L0_gnn_Wv).T), "bv": _head_bias(to(L0_gnn_bv))[None, :],
    })
    late = _pack(LATE, LATE_W, {
        "wo": to(L0_gnn_Wo).T, "bo": to(L0_gnn_bo)[None, :],
        "iota": cols, "tile_of": cols // P, "ones": np.ones((P, P), np.float32),
        "row_no": rows + P * np.arange(C, dtype=np.float32), "in_group": rows % RPG,
        "group_of": rows // RPG + P // RPG * np.arange(C, dtype=np.float32),
        "cap": np.where(rows < E, 2.0 * N, (rows - E + 1) * P),
        "wi": to(L0_ffn_Wi).T, "bi": to(L0_ffn_bi).reshape(KH, P).T,
        "ws": to(L0_ffn_Ws)[:, 0].transpose(2, 0, 1).reshape(KH, P, L, HID).transpose(1, 2, 0, 3).reshape(P, -1),
        "fwo": to(L0_ffn_Wo).T.reshape(KH, P, D).transpose(1, 0, 2).reshape(P, KH * D),
        "fbo": to(L0_ffn_bo)[None, :],
    })
    route = to(L0_ffn_route_id)
    adj = to(adj)
    arrays = {
        "x": to(x), "early": early, "late": late, "adj": adj, "adjT": adj.T,
        "route_tok": np.repeat(route, RPG).reshape(C, P).T, "route_row": route[None, :],
        "br": to(L0_ffn_br).transpose(1, 0, 2).reshape(E, L * HID),
        "bs": to(L0_ffn_bs).reshape(1, L * HID),
        "wr": to(L0_ffn_Wr).transpose(0, 3, 1, 2).reshape(L, KH, P, E, HID).transpose(0, 2, 3, 1, 4).reshape(L, P, -1),
    }
    nc = bacc.Bacc("TRN2", target_bir_lowering=False, num_devices=1)
    given, args = {}, []
    for name, a in arrays.items():
        given[f"in_{name}"] = np.ascontiguousarray(a)
        args.append(nc.dram_tensor(f"in_{name}", a.shape, mybir.dt.from_np(a.dtype), kind="ExternalInput").ap())
    out = nc.dram_tensor("out", (N, D), F32, kind="ExternalOutput").ap()
    gnn_ffn_kernel(nc, *args, out)
    return run_bass_kernel_spmd(nc, [given], core_ids=[0]).results[0]["out"]
```

```python
from contextlib import ExitStack

import numpy as np

import concourse.bass as bass
from concourse import mybir

ALU = mybir.AluOpType
ACT = mybir.ActivationFunctionType
F32 = mybir.dt.float32
BF16 = mybir.dt.bfloat16
I32 = mybir.dt.int32
F32R = mybir.dt.float32r

P = 128
N = 512
D = 128
C = N // P
H = 8
DH = D // H
HS = 32
HG = P // HS
G = H // HG
HID = 256
KH = HID // P
L = 2
E = 16
GR = 64
RPG = N // GR
PAIRS = E + C - 1
LAST = PAIRS - C + 1
EPS = 1e-5
NEG = -1e30
FLOOR = -1e15
TINY = 1e-30
BLOCKS = ((0, 0), (0, 1), (1, 0))
MROW = len(BLOCKS) * DH
SROWS = 96
MP = H // 2
UNITS = 2 * C
STEPS = MP * C
SLOTS = 8
MAXBANKS = 3
EXPBANK = 3
OUTBANK = 7
FIRST = 2
GROUPS = ((2, 4), (4, 8))
QROWS = (H - FIRST) * DH
WPARTS = 4
WARM = 10
KEEP_WARM = 4
NORM_WARM = 8

EARLY = {}
MIDDLE = {}
LATE = {}


def _columns(table, fields):
    at = 0
    for name, width in fields:
        table[name] = (at, at + width)
        at += width
    return at


EARLY_W = _columns(EARLY, [("ident", P), ("wk", D), ("bk", 1), ("hnT", N), ("ET", 2),
                           ("wq_first", FIRST * MROW), ("bq_first", FIRST), ("wq", QROWS), ("bq", 1)])
MIDDLE_W = _columns(MIDDLE, [("wv", G * P), ("bv", G * P)])
LATE_W = _columns(LATE, [("wo", D), ("bo", D), ("iota", N), ("tile_of", N), ("row_no", C), ("group_of", C),
                         ("in_group", 1), ("cap", 1), ("wi", HID), ("bi", KH), ("ws", L * KH * HID),
                         ("fwo", KH * D), ("fbo", D)])

RING = []
for _n in range(MP * UNITS):
    RING.append(("unit", _n))
    if _n % UNITS == 1 and _n > UNITS:
        RING.append(("turn", _n // UNITS - 1))
RING.append(("turn", MP - 1))
BANK_OF = {entry: _i % MAXBANKS for _i, entry in enumerate(RING)}
FILLS = [1, 2, 2, 3, 1, 1, 2, 3, 3, 1]
_upto = [2 * UNITS + 1 + sum(FILLS[:_s + 1]) for _s in range(len(FILLS))]
TURNED_AFTER = [next(_s for _s, _n in enumerate(_upto) if RING.index(("turn", _p)) < _n) for _p in range(1, MP)]
ADD_VALUES = [[6, 7, 8, 9], [14, 15, 15, 16]]
TURN_OUTPUTS_AFTER = 12
VALUES_AFTER = [UNITS + 3, UNITS + 5]
PAIRS_AFTER = 12
STORED = [slice(0, C - 1), slice(C - 1, C)]
ACCBANK = [4, 0]


def gnn_ffn_kernel(nc, x, early, middle, late, adj, adjT, route_tok, route_row, br, bs, wr, out):
    with ExitStack() as ctx:
        def sb(name, shape, dt=F32):
            return ctx.enter_context(nc.sbuf_tensor(name, shape, dt))

        def sem(name):
            return ctx.enter_context(nc.semaphore(name))

        xs = sb("xs", [P, C, D])
        ea = sb("ea", [P, EARLY_W])
        ma = sb("ma", [P, MIDDLE_W])
        la = sb("la", [P, LATE_W])
        warm = sb("warm", [P, N], BF16)
        with nc.sbuf_tensor("adj_i", [P, C, N], I32) as adj_i, nc.sbuf_tensor("adjT_i", [P, C, N], I32) as adjT_i:
            pass
        gather = sb("gather", [P, C, N], F32R)
        scatter = sb("scatter", [P, C, N], F32R)
        mask = sb("mask", [P, C, N], BF16)
        maskT = sb("maskT", [P, C, N], BF16)
        ident_b = sb("ident_b", [P, P], BF16)
        stats = sb("stats", [P, C, 6])
        mv = sb("mv", [P, C, 2])
        var_eps = sb("var_eps", [P, C])
        rstd = sb("rstd", [P, C])
        half = sb("half", [P, C])
        xn = sb("xn", [P, C, D])
        xnT = sb("xnT", [P, N])
        hT = [sb("hT0", [P, KH, N])]
        with nc.sbuf_tensor("msgT", [P, N], F32) as msgT, nc.sbuf_tensor("junk", [P, 2, N], BF16) as junk:
            pass
        hT.append(sb("hT1", [P, KH, N]))
        with nc.sbuf_tensor("v", [P, C, G * P], F32) as v:
            pass
        hT.append(sb("hT2", [P, KH, N]))
        with nc.sbuf_tensor("q_part", [P, 2, N], F32R) as q_part, nc.sbuf_tensor("k_part", [P, 2, N], F32R) as k_part:
            pass
        zT_part = sb("zT_part", [P, 2, N], F32R)
        wi_part = sb("wi_part", [P, 2, HID], F32R)
        sb("rest_of_k_part", [P, 2, N - HID])
        m_part = sb("m_part", [UNITS, MP, 2, P], F32R)
        maxima = sb("maxima", [P, MP, 2, C])
        oT = sb("oT", [P, N])
        den = sb("den", [P, G, C, HG])
        rden = sb("rden", [P, G, C, HG])
        on = sb("on", [P, C, D])
        onT = sb("onT", [P, N])
        x_bo = sb("x_bo", [P, C, D])
        x2 = sb("x2", [P, C, D])
        x2_bo = sb("x2_bo", [P, C, D])
        z = sb("z", [P, C, D])
        route_t = sb("route_t", [P, C], I32)
        route_r = sb("route_r", [P, GR], I32)
        key_r = sb("key_r", [P, GR])
        key_t = sb("key_t", [P, C])
        less = sb("less", [P, C + 1, GR])
        slot_g = sb("slot_g", [P, C])
        slot = sb("slot", [P, C])
        count = sb("count", [P, 1])
        first = sb("first", [P, 1])
        past = sb("past", [P, N], F32R)
        ones_r = sb("ones_r", [P, P], F32R)
        pair_r = sb("pair_r", [P, N])
        onehot = sb("onehot", [P, N], F32R)
        turn = sb("turn", [1, 2, PAIRS])
        window = sb("window", [1, PAIRS], I32)
        slot_d = sb("slot_d", [P, C, P], F32R)
        slot_r = sb("slot_r", [P, N])
        br_s = sb("br_s", [E, L * HID])
        bs_s = sb("bs_s", [E, L * HID])
        bias = sb("bias", [E, L * HID])
        bias_part = sb("bias_part", [P, 2, L * HID], F32R)
        with nc.sbuf_tensor("q_stack", [P, H, N], F32R) as q_stack, \
                nc.sbuf_tensor("k_stack", [P, H, N], F32R) as k_stack:
            pass
        w = [sb("w1", [P, E * KH * HID])]
        w.insert(0, sb("w0", [P, E * KH * HID]))
        with nc.sbuf_tensor("pT", [P, SLOTS, 2, N], F32) as pT:
            pass
        z_part = sb("z_part", [P, 2, C, D], F32R)
        hs = sb("hs", [P, C, HID])
        hs_part = sb("hs_part", [P, 2, C, HID], F32R)
        picked = sb("picked", [P, 3, KH, P])
        res = sb("res", [P, C, D])
        ps = ctx.enter_context(nc.psum_tensor("ps", [P, 8, N], F32))

        def e_(name):
            a, b = EARLY[name]
            return ea[:, a:b]

        def m_(name):
            a, b = MIDDLE[name]
            return ma[:, a:b]

        def l_(name):
            a, b = LATE[name]
            return la[:, a:b]

        ident = e_("ident")
        ws = l_("ws").rearrange("p (l k h) -> p l k h", l=L, k=KH)
        fwo = l_("fwo").rearrange("p (k d) -> p k d", k=KH)
        wi = l_("wi")

        def window_of(engine, i):
            return nc.values_load(window[0:1, i:i + 1], engines=(engine,), min_val=max(0, i - E + 1),
                                  max_val=min(i, C - 1),
                                  skip_runtime_bounds_check_because="a pair's number is its expert plus its window")

        x_in = sem("x_in")
        early_in = sem("early_in")
        adj_in = sem("adj_in")
        adjT_in = sem("adjT_in")
        middle_in = sem("middle_in")
        warm_ready = sem("warm_ready")
        ones_ready = sem("ones_ready")
        late_in = sem("late_in")
        route_in = sem("route_in")
        bias_in = sem("bias_in")
        w_in = [[sem(f"w{l}_{n}_in") for n in range(WPARTS)] for l in range(L)]
        out_done = sem("out_done")
        dve_step = sem("dve_step")
        pool_step = sem("pool_step")
        var_ready = sem("var_ready")
        rstd_ready = sem("rstd_ready")
        xn_ready = sem("xn_ready")
        xnT_psum = sem("xnT_psum")
        xnT_ready = sem("xnT_ready")
        msgT_ready = sem("msgT_ready")
        k_psum = sem("k_psum")
        v_psum = sem("v_psum")
        v_ready = sem("v_ready")
        q_psum = sem("q_psum")
        maskT_ready = sem("maskT_ready")
        ident_b_ready = sem("ident_b_ready")
        stack_rows = sem("stack_rows")
        k_stacked = sem("k_stacked")
        q_stacked = [sem(f"q{group}_stacked") for group in range(len(GROUPS))]
        m_psum = sem("m_psum")
        m_high = sem("m_high")
        m_low = sem("m_low")
        m_stacked = sem("m_stacked")
        first_psum = sem("first_psum")
        first_high = sem("first_high")
        first_low = sem("first_low")
        k_high = sem("k_high")
        k_low = sem("k_low")
        q_high = sem("q_high")
        q_low = sem("q_low")
        max_psum = sem("max_psum")
        max_read = sem("max_read")
        exp_psum = sem("exp_psum")
        exp_ready = sem("exp_ready")
        pv_done = sem("pv_done")
        oT_ready = sem("oT_ready")
        o_psum = sem("o_psum")
        on_ready = sem("on_ready")
        onT_psum = sem("onT_psum")
        onT_ready = sem("onT_ready")
        attn_psum = sem("attn_psum")
        x_bo_ready = sem("x_bo_ready")
        x2_ready = sem("x2_ready")
        wi_ready = sem("wi_ready")
        x2_bo_ready = sem("x2_bo_ready")
        z_ready = sem("z_ready")
        slot_ready = sem("slot_ready")
        past_ready = sem("past_ready")
        pair_psum = sem("pair_psum")
        pair_ready = sem("pair_ready")
        window_ready = sem("window_ready")
        onehot_ready = sem("onehot_ready")
        gather_ready = sem("gather_ready")
        slot_d_ready = sem("slot_d_ready")
        slot_r_psum = sem("slot_r_psum")
        slot_r_ready = sem("slot_r_ready")
        scatter_ready = sem("scatter_ready")
        w_ready = [sem(f"w{l}_ready") for l in range(L)]
        bias_ready = sem("bias_ready")
        zT_psum = sem("zT_psum")
        zT_high = sem("zT_high")
        zT_low = sem("zT_low")
        h0_psum = sem("h0_psum")
        h0_act = sem("h0_act")
        h0_dve = sem("h0_dve")
        picked_ready = sem("picked_ready")
        pair_done = sem("pair_done")
        h_ready = sem("h_ready")
        h_turned = sem("h_turned")
        hT_ready = sem("hT_ready")
        z_high = sem("z_high")
        z_low = sem("z_low")
        h_low = sem("h_low")
        unsorted_psum = sem("unsorted_psum")
        unsorted_act = sem("unsorted_act")
        unsorted_dve = sem("unsorted_dve")
        out_psum = sem("out_psum")
        res_ready = sem("res_ready")

        halves = (slice(0, N // 2), slice(N // 2, N))

        block = ctx.enter_context(nc.Block())

        @block.sync
        def _(sp):
            sp.dma_start(xs[:], x.rearrange("(c p) d -> p c d", p=P)).then_inc(x_in, 16)
            sp.dma_start(ea[:], early).then_inc(early_in, 16)
            sp.dma_start(adj_i[:], adj.rearrange("(c p) n -> p c n", p=P)).then_inc(adj_in, 16)

            def stack(dst, src, side, part, signal, heads=slice(0, H)):
                for n, parts in enumerate(BLOCKS):
                    if parts[side] == part:
                        sp.dma_start(dst[n * DH:(n + 1) * DH, heads, :].bitcast(F32),
                                     src.bitcast(F32)).then_inc(signal, 16)

            def stack_queries(part, group):
                lo, hi = GROUPS[group]
                stack(q_stack, q_part[(lo - FIRST) * DH:(hi - FIRST) * DH, part, :], 0, part, q_stacked[group],
                      slice(lo, hi))

            part = E // WPARTS * KH * HID

            def load_weights(l, n):
                cols = slice((WPARTS - 1 - n) * part, (WPARTS - n) * part)
                sp.dma_start(w[l][:, cols], wr[l, :, cols]).then_inc(w_in[l][n], 16)

            sp.wait_ge(stack_rows, 1)
            sp.wait_ge(k_high, 1)
            stack(k_stack, k_part[:, 0, :], 1, 0, k_stacked)
            sp.wait_ge(k_low, 1)
            stack(k_stack, k_part[:, 1, :], 1, 1, k_stacked)
            sp.wait_ge(stack_rows, 2)
            sp.dma_start(adjT_i[:], adjT.rearrange("(c p) n -> p c n", p=P)).then_inc(adjT_in, 16)
            sp.dma_start(ma[:], middle).then_inc(middle_in, 16)
            sp.wait_ge(q_high, 1)
            stack_queries(0, 0)
            sp.wait_ge(q_low, 1)
            stack_queries(1, 0)
            stack_queries(0, 1)
            stack_queries(1, 1)
            sp.dma_start(la[:], late).then_inc(late_in, 16)
            sp.dma_start(route_t[:], route_tok).then_inc(route_in, 16)
            sp.dma_start(route_r[:], route_row.to_broadcast([P, GR])).then_inc(route_in, 16)
            for p in range(MP):
                for n in range(2):
                    sp.wait_ge(m_low if n else m_high, p + 1)
                    sp.dma_start(q_stack[MROW + n:MROW + n + 1, 2 * p:2 * p + 2, :].bitcast(F32),
                                 m_part[:, p, n, :].bitcast(F32)).then_inc(m_stacked, 16)
                if p == 0:
                    sp.dma_start(br_s[:], br).then_inc(bias_in, 16)
                    sp.dma_start(bs_s[:], bs.to_broadcast([E, L * HID])).then_inc(bias_in, 16)
                load_weights(0, p)
            sp.wait_ge(exp_psum, STEPS)
            for n in range(WPARTS):
                load_weights(1, n)
            for n, rows in enumerate(STORED):
                sp.wait_ge(res_ready, n + 1)
                sp.dma_start(out.rearrange("(c p) d -> p c d", p=P)[:, rows, :], res[:, rows, :]).then_inc(out_done, 16)
            sp.wait_ge(out_done, 2 * 16)

        @block.gpsimd
        def _(pool):
            steps = [0]

            def link(ins):
                steps[0] += 1
                ins.then_inc(pool_step, 1)
                pool.wait_ge(pool_step, steps[0])

            link(nc.gpsimd.memset(half[:], -0.5))
            nc.gpsimd.memset(k_stack[0:SROWS, :, :].bitcast(F32), -1.0).then_inc(stack_rows, 1)
            pool.wait_ge(var_ready, 1)
            nc.gpsimd.tensor_tensor(rstd[:], var_eps[:], half[:], ALU.pow).then_inc(rstd_ready, 1)
            nc.gpsimd.memset(q_stack[0:SROWS, :, :].bitcast(F32), 0.0).then_inc(stack_rows, 1)
            pool.wait_ge(early_in, 16)
            nc.gpsimd.tensor_copy(ident_b[:], ident).then_inc(ident_b_ready, 1)
            pool.wait_ge(adjT_in, 16)
            for a in range(C):
                nc.gpsimd.tensor_scalar(maskT[:, a, :], adjT_i[:, a, :], 0.0, NEG,
                                        ALU.is_equal, ALU.mult).then_inc(maskT_ready, 1)
            pool.wait_ge(late_in, 16)
            pool.wait_ge(x_in, 16)
            for c in range(C):
                ins = nc.gpsimd.tensor_tensor(x_bo[:, c, :], xs[:, c, :], l_("bo"), ALU.add)
            ins.then_inc(x_bo_ready, 1)
            for l in range(L):
                for k in range(KH):
                    cols = slice(k * P, (k + 1) * P)
                    link(nc.gpsimd.tensor_tensor(ws[:, l, k, cols], ws[:, l, k, cols], ident, ALU.add))

            def add_shared(l, parts=range(WPARTS)):
                part = E // WPARTS
                for n in parts:
                    pool.wait_ge(w_in[l][n], 16)
                    at = w[l][:].rearrange("p (n e c) -> p n e c", n=WPARTS, e=part)[:, WPARTS - 1 - n]
                    shared = ws[:, l].rearrange("p k h -> p (k h)").unsqueeze(1).to_broadcast([P, part, KH * HID])
                    nc.gpsimd.tensor_tensor(at, at, shared, ALU.add).then_inc(w_ready[l], 1)

            add_shared(0, range(WPARTS - 1))
            pool.wait_ge(slot_ready, 1)
            for c in range(C):
                ins = nc.gpsimd.tensor_scalar(slot_d[:, c, :], ident, slot[:, c:c + 1], None, ALU.mult)
            ins.then_inc(slot_d_ready, 1)
            for c in range(C):
                ins = nc.gpsimd.tensor_scalar(gather[:, c, :], l_("iota"), slot[:, c:c + 1], None, ALU.is_equal)
            ins.then_inc(gather_ready, 1)
            add_shared(0, range(WPARTS - 1, WPARTS))
            pool.wait_ge(var_ready, 2)
            nc.gpsimd.tensor_tensor(rstd[:], var_eps[:], half[:], ALU.pow).then_inc(rstd_ready, 1)
            add_shared(1)
            pool.wait_ge(x2_ready, 1)
            for c in range(C):
                ins = nc.gpsimd.tensor_tensor(x2_bo[:, c, :], x2[:, c, :], l_("fbo"), ALU.add)
            ins.then_inc(x2_bo_ready, 1)
            pool.wait_ge(slot_r_ready, 1)
            for c in range(C):
                a = LATE["row_no"][0] + c
                ins = nc.gpsimd.tensor_scalar(scatter[:, c, :], slot_r[:], la[:, a:a + 1], None, ALU.is_equal)
            ins.then_inc(scatter_ready, 1)

        @block.scalar
        def _(act):
            act.preload_act_table(ACT.Exp)
            act.wait_ge(early_in, 16)
            act.wait_ge(k_psum, 1)
            nc.scalar.activation(k_part[:, 0, :], ps[:, 1, :], ACT.Identity, bias=e_("bk")).then_inc(k_high, 1)
            act.wait_ge(xnT_psum, 1)
            nc.scalar.activation(xnT[:], ps[:, 0, :], ACT.Identity).then_inc(xnT_ready, 1)
            act.wait_ge(stack_rows, 2)
            for h in range(FIRST):
                act.wait_ge(first_psum, h + 1)
                nc.scalar.activation(q_stack[0:MROW, h, :], ps[0:MROW, EXPBANK + h, :], ACT.Identity,
                                     bias=e_("bq_first")[0:MROW, h:h + 1]).then_inc(first_high, 1)
            act.wait_ge(q_psum, 1)
            nc.scalar.activation(q_part[0:QROWS, 0, :], ps[0:QROWS, 2, :], ACT.Identity, bias=e_("bq")[0:QROWS, :])\
                .then_inc(q_high, 1)

            def maxima_high(p):
                act.wait_ge(m_psum, p + 1)
                nc.scalar.activation(m_part[:, p, 0, :], ps[0:UNITS, BANK_OF["turn", p], 0:P], ACT.Identity)\
                    .then_inc(m_high, 1)

            maxima_high(0)
            for s in range(STEPS):
                for p in range(1, MP):
                    if s == TURNED_AFTER[p - 1]:
                        maxima_high(p)
                act.wait_ge(exp_psum, s + 1)
                if s >= SLOTS:
                    p, a = divmod(s - SLOTS, C)
                    act.wait_ge(pv_done, p // 2 * C + a + 1)
                bank = EXPBANK + s % 2 * 2
                nc.scalar.activation(pT[:, s % SLOTS, :, :], ps[:, bank:bank + 2, :], ACT.Exp,
                                     scale=DH ** -0.5).then_inc(exp_ready, 1)
                if s == ADD_VALUES[0][-1] + 1:
                    act.wait_ge(pv_done, C)
                    nc.scalar.activation(oT[:], ps[:, OUTBANK, :], ACT.Identity).then_inc(oT_ready, 1)
            act.wait_ge(pv_done, G * C)
            act.wait_ge(o_psum, 1)
            nc.scalar.activation(oT[:], ps[:, OUTBANK, :], ACT.Identity).then_inc(oT_ready, 1)
            act.wait_ge(onT_psum, 1)
            nc.scalar.activation(onT[:], ps[:, 0, :], ACT.Identity).then_inc(onT_ready, 1)
            act.wait_ge(slot_r_psum, 1)
            nc.scalar.activation(slot_r[:], ps[:, 2, :], ACT.Identity).then_inc(slot_r_ready, 1)
            for c in range(C):
                act.wait_ge(z_ready, c + 1)
                nc.scalar.activation(z_part[:, 0, c, :], z[:, c, :], ACT.Identity).then_inc(z_high, 1)
            nc.scalar.activation(x2[:].rearrange("p c d -> p (c d)"), ps[:, 1, :], ACT.Identity).then_inc(x2_ready, 1)
            act.wait_ge(zT_psum, 1)
            nc.scalar.activation(zT_part[:, 0, :], ps[:, 2, :], ACT.Identity).then_inc(zT_high, 1)
            act.wait_ge(h0_psum, 1)
            for rows in (slice(0, P), slice(P, N)):
                nc.scalar.activation(hT[0][:, 0, rows], ps[:, 3, rows], ACT.Relu, bias=l_("bi")[:, 0:1])\
                    .then_inc(h0_act, 1)
            for l in range(L):
                for t in range(C):
                    act.wait_ge(pair_done, l * PAIRS + LAST + t)
                    h_out = hs[:, t, :] if l < L - 1 else hs_part[:, 0, t, :]
                    nc.scalar.activation(h_out, ps[:, ACCBANK[l] + t, 0:HID], ACT.Relu).then_inc(h_ready, 1)
            act.wait_ge(unsorted_psum, 1)
            for rows in halves:
                nc.scalar.activation(hT[L][:, 0, rows], ps[:, 4, rows], ACT.Identity).then_inc(unsorted_act, 1)

        @block.vector
        def _(dve):
            steps = [0]

            def link(ins):
                steps[0] += 1
                ins.then_inc(dve_step, 1)
                dve.wait_ge(dve_step, steps[0])

            def statistics(src):
                for c in range(C):
                    ins = nc.vector.bn_stats(stats[:, c, :], src[:, c, :])
                link(ins)
                for c in range(C):
                    ins = nc.vector.bn_aggr(mv[:, c, :], stats[:, c, :])
                link(ins)
                nc.vector.tensor_scalar(var_eps[:], mv[:, :, 1], EPS, None, ALU.add).then_inc(var_ready, 1)

            def normed(src, dst, c):
                return nc.vector.tensor_scalar(dst[:, c, :], src[:, c, :], mv[:, c, 0:1], rstd[:, c:c + 1],
                                               ALU.subtract, ALU.mult)

            nc.vector.memset(warm[:], 0.0).then_inc(warm_ready, 1)
            link(nc.vector.memset(bias_part[:].bitcast(F32), 0.0))
            nc.vector.memset(ones_r[:].bitcast(F32), 1.0).then_inc(ones_ready, 1)
            dve.wait_ge(x_in, 16)
            statistics(xs)
            dve.wait_ge(early_in, 16)
            a = EARLY["ET"][0] + 1
            nc.vector.tensor_scalar(msgT[:], e_("hnT"), ea[:, a:a + 1], None, ALU.add).then_inc(msgT_ready, 1)
            dve.wait_ge(rstd_ready, 1)
            for c in range(C):
                normed(xs, xn, c).then_inc(xn_ready, 1)

            def low_part(bank, bias_, low, high, signal, rows=slice(0, P)):
                nc.vector.scalar_tensor_tensor(low, ps[rows, bank, :], bias_, high.bitcast(F32),
                                               ALU.add, ALU.subtract).then_inc(signal, 1)

            dve.wait_ge(k_high, 1)
            low_part(1, e_("bk"), k_part[:, 1, :], k_part[:, 0, :], k_low)
            dve.wait_ge(adj_in, 16)
            link(nc.vector.tensor_scalar(mask[:], adj_i[:], 0.0, NEG, ALU.is_equal, ALU.mult))
            low_rows = slice(2 * DH, 3 * DH)
            for h in range(FIRST):
                dve.wait_ge(first_high, h + 1)
                low_part(EXPBANK + h, e_("bq_first")[low_rows, h:h + 1], q_stack[low_rows, h, :],
                         q_stack[low_rows, h, :], first_low, low_rows)
            dve.wait_ge(q_high, 1)
            low_part(2, e_("bq")[0:QROWS, :], q_part[0:QROWS, 1, :], q_part[0:QROWS, 0, :], q_low, slice(0, QROWS))

            def pair_max(p):
                for c in range(C):
                    for j in range(2):
                        n = p * UNITS + c * 2 + j
                        if p > 0 and c == 1 and j == 0:
                            maxima_low(p - 1)
                        if n in VALUES_AFTER:
                            values(VALUES_AFTER.index(n))
                        dve.wait_ge(max_psum, n + 1)
                        if n >= 2:
                            dve.wait_ge(max_read, n - 1)
                        nc.vector.tensor_tensor_reduce(junk[:, n % 2, :], ps[:, BANK_OF["unit", n], :], mask[:, c, :],
                                                       1.0, FLOOR, ALU.add, ALU.max,
                                                       maxima[:, p, j, c:c + 1]).then_inc(max_read, 1)

            def maxima_low(p):
                dve.wait_ge(m_high, p + 1)
                nc.vector.tensor_tensor(m_part[:, p, 1, :], ps[0:UNITS, BANK_OF["turn", p], 0:P],
                                        m_part[:, p, 0, :].bitcast(F32), ALU.subtract).then_inc(m_low, 1)

            def values(b):
                dve.wait_ge(v_psum, 2 * b + 2)
                nc.vector.tensor_tensor(
                    v[:, 2 * b:2 * b + 2, :], ps[:, EXPBANK + b, :].rearrange("p (a m) -> p a m", a=2),
                    m_("bv").unsqueeze(1).to_broadcast([P, 2, G * P]), ALU.add).then_inc(v_ready, 1)

            def routing():
                dve.wait_ge(route_in, 32)
                dve.wait_ge(late_in, 16)
                nc.vector.scalar_tensor_tensor(key_r[:], route_r[:], float(GR), l_("iota")[:, 0:GR],
                                               ALU.mult, ALU.add)
                link(nc.vector.scalar_tensor_tensor(key_t[:], route_t[:], float(GR), l_("group_of"),
                                                    ALU.mult, ALU.add))
                for c in range(C):
                    ins = nc.vector.tensor_scalar(less[:, c, :], key_r[:], key_t[:, c:c + 1], None,
                                                  ALU.is_lt, ALU.add, accum_out=slot_g[:, c:c + 1])
                link(ins)
                nc.vector.tensor_scalar(slot[:], slot_g[:], float(RPG), l_("in_group"),
                                        ALU.mult, ALU.add).then_inc(slot_ready, 1)
                link(nc.vector.tensor_scalar(less[:, C, :], route_r[:, :], l_("row_no")[:, 0:1], None,
                                             ALU.is_le, ALU.add, accum_out=count[:, :]))
                link(nc.vector.tensor_scalar(first[:, :], count[:, :], float(RPG), l_("cap")[:, :],
                                             ALU.mult, ALU.min))
                nc.vector.tensor_scalar(past[:, :], l_("iota")[:, :], first[:, :], None,
                                        ALU.is_ge).then_inc(past_ready, 1)

            def pair_table():
                dve.wait_ge(pair_psum, 1)
                nc.vector.tensor_copy(pair_r[:], ps[:, 1, :]).then_inc(pair_ready, 1)
                dve.wait_ge(pair_ready, 1)
                nc.vector.scalar_tensor_tensor(onehot[:], pair_r[:], l_("row_no")[:, 0:1],
                                               l_("tile_of"), ALU.subtract, ALU.is_equal)\
                    .then_inc(onehot_ready, 1)
                numbers = l_("iota")[0:1, 0:PAIRS]
                link(nc.vector.tensor_scalar(turn[:, 0, :], numbers, pair_r[0:1, P:P + 1], None, ALU.is_ge))
                link(nc.vector.scalar_tensor_tensor(turn[:, 1, :], numbers, pair_r[0:1, 2 * P:2 * P + 1],
                                                    turn[:, 0, :], ALU.is_ge, ALU.add))
                nc.vector.scalar_tensor_tensor(window[:, :], numbers, pair_r[0:1, 3 * P:3 * P + 1],
                                               turn[:, 1, :], ALU.is_ge, ALU.add).then_inc(window_ready, 1)

            def biases():
                dve.wait_ge(bias_in, 32)
                link(nc.vector.tensor_tensor(bias[:], br_s[:], bs_s[:], ALU.add))
                link(nc.vector.tensor_copy(bias_part[0:E, 0, :], bias[:]))
                nc.vector.tensor_tensor(bias_part[0:E, 1, :], bias[:], bias_part[0:E, 0, :].bitcast(F32),
                                        ALU.subtract).then_inc(bias_ready, 1)

            def normalize(g):
                dve.wait_ge(o_psum, g + 1)
                o = ps[:, OUTBANK, :].rearrange("p (c j m) -> p c j m", c=C, j=HG)
                link(nc.vector.tensor_scalar(den[:, g], o[:, :, :, DH], TINY, None, ALU.max))
                link(nc.vector.reciprocal(rden[:, g], den[:, g]))
                on_g = on[:].rearrange("p c (g j d) -> p g c j d", g=G, j=HG)[:, g]
                ins = nc.vector.tensor_tensor(on_g, o[:, :, :, 0:DH],
                                              rden[:, g].unsqueeze(3).to_broadcast([P, C, HG, DH]), ALU.mult)
                ins.then_inc(on_ready, 1)

            pair_max(0)
            pair_max(1)
            pair_max(2)
            pair_max(3)
            maxima_low(3)
            routing()
            normalize(0)
            biases()
            pair_table()
            nc.vector.tensor_copy(wi_part[:, 0, :], wi).then_inc(wi_ready, 1)
            dve.wait_ge(wi_ready, 1)
            nc.vector.tensor_tensor(wi_part[:, 1, :], wi, wi_part[:, 0, :].bitcast(F32),
                                    ALU.subtract).then_inc(wi_ready, 1)
            normalize(1)
            dve.wait_ge(attn_psum, 1)
            rows_x2 = ps[:, 1, :].rearrange("p (c d) -> p c d", c=C)
            statistics(rows_x2)
            dve.wait_ge(rstd_ready, 2)
            for c in range(C):
                normed(rows_x2, z, c).then_inc(z_ready, 1)
            for c in range(C):
                dve.wait_ge(z_high, c + 1)
                nc.vector.tensor_tensor(z_part[:, 1, c, :], z[:, c, :], z_part[:, 0, c, :].bitcast(F32),
                                        ALU.subtract).then_inc(z_low, 1)
            dve.wait_ge(zT_psum, 2)
            nc.vector.tensor_copy(zT_part[:, 1, :], ps[:, 0, :]).then_inc(zT_low, 1)
            dve.wait_ge(h0_psum, 2)

            def h0_rows(rows):
                nc.vector.tensor_scalar(hT[0][:, 1, rows], ps[:, 2, rows], l_("bi")[:, 1:2], 0.0,
                                        ALU.add, ALU.max).then_inc(h0_dve, 1)

            h0_rows(slice(0, P))
            dve.wait_ge(h0_act, 1)
            dve.wait_ge(h0_dve, 1)

            def turned(l, t):
                dve.wait_ge(h_turned, l * C + t + 1)
                nc.vector.tensor_copy(hT[l + 1][:, :, t * P:(t + 1) * P],
                                      ps[:, ACCBANK[l] + t, HID:2 * HID].rearrange("p (k s) -> p k s", k=KH))\
                    .then_inc(hT_ready, 1)

            dve.wait_ge(window_ready, 1)
            for l in range(L):
                for i in range(PAIRS):
                    n = l * PAIRS + i
                    t = window_of(mybir.EngineType.DVE, i)
                    if l > 0 and i < C:
                        turned(l - 1, i)
                        dve.wait_ge(hT_ready, (l - 1) * C + i + 1)
                    if n == 1:
                        h0_rows(slice(P, N))
                        dve.wait_ge(h0_dve, 2)
                        dve.wait_ge(h0_act, 2)
                    if n >= 3:
                        dve.wait_ge(pair_done, n - 2)
                    nc.vector.scalar_tensor_tensor(picked[:, n % 3],
                                                   pair_r[:, bass.ds(t * P, P)].unsqueeze(1).to_broadcast([P, KH, P]),
                                                   float(i),
                                                   hT[l][:, :, bass.ds(t * P, P)], ALU.is_equal, ALU.mult)\
                        .then_inc(picked_ready, 1)
            for t in range(C):
                dve.wait_ge(h_ready, (L - 1) * C + t + 1)
                nc.vector.scalar_tensor_tensor(hs_part[:, 1, t, :], ps[:, ACCBANK[L - 1] + t, 0:HID], 0.0,
                                               hs_part[:, 0, t, :].bitcast(F32), ALU.max, ALU.subtract)\
                    .then_inc(h_low, 1)
            dve.wait_ge(unsorted_psum, 2)
            for rows in halves:
                nc.vector.tensor_copy(hT[L][:, 1, rows], ps[:, 5, rows]).then_inc(unsorted_dve, 1)
            dve.wait_ge(x2_bo_ready, 1)
            for n, rows in enumerate(STORED):
                dve.wait_ge(out_psum, n + 1)
                nc.vector.tensor_tensor(res[:, rows, :], ps[:, 6 + n, 0:len(range(C)[rows]) * D]
                                        .rearrange("p (c d) -> p c d", d=D),
                                        x2_bo[:, rows, :], ALU.add).then_inc(res_ready, 1)

        @block.tensor
        def _(pe):
            def mm(o, a, b, start=True, stop=True, pos=None):
                return nc.tensor.matmul(o, a, b, start=start, stop=stop, skip_group_check=True, tile_position=pos)

            def hold_clock(times, bank=OUTBANK):
                for _ in range(times):
                    mm(ps[:, bank, :], warm[:, 0:P], warm[:])

            pe.wait_ge(warm_ready, 1)
            hold_clock(WARM)
            pe.wait_ge(msgT_ready, 1)
            mm(ps[:, 1, :], e_("wk"), msgT[:]).then_inc(k_psum, 1)
            for c in range(C):
                pe.wait_ge(xn_ready, c + 1)
                ins = nc.tensor.transpose(ps[:, 0, c * P:(c + 1) * P], xn[:, c, :], ident)
            ins.then_inc(xnT_psum, 1)
            pe.wait_ge(xnT_ready, 1)
            for h in range(FIRST):
                mm(ps[0:MROW, EXPBANK + h, :], e_("wq_first")[:, h * MROW:(h + 1) * MROW], xnT[:])\
                    .then_inc(first_psum, 1)
            mm(ps[0:QROWS, 2, :], e_("wq"), xnT[:]).then_inc(q_psum, 1)

            def values(a):
                pe.wait_ge(middle_in, 16)
                mm(ps[:, EXPBANK + a // 2, (a % 2) * G * P:(a % 2 + 1) * G * P], msgT[:, a * P:(a + 1) * P],
                   m_("wv")).then_inc(v_psum, 1)

            def fill(i):
                kind, n = RING[i]
                if i == 2:
                    pe.wait_ge(q_low, 1)
                if i >= MAXBANKS:
                    was, m = RING[i - MAXBANKS]
                    pe.wait_ge(max_read if was == "unit" else m_low, m + 1)
                if kind == "unit":
                    p, cj = divmod(n, UNITS)
                    c, h = cj // 2, 2 * p + cj % 2
                    for group, (lo, _) in enumerate(GROUPS):
                        if n == lo // 2 * UNITS:
                            pe.wait_ge(q_stacked[group], 16 * len(BLOCKS))
                    mm(ps[:, i % MAXBANKS, :], q_stack[0:SROWS, h, c * P:(c + 1) * P], k_stack[0:SROWS, h, :])\
                        .then_inc(max_psum, 1)
                else:
                    pe.wait_ge(max_read, (n + 1) * UNITS)
                    nc.tensor.transpose(ps[0:UNITS, i % MAXBANKS, 0:P], maxima[:, n].rearrange("p j c -> p (j c)"),
                                        ident).then_inc(m_psum, 1)

            def add_mask(s):
                if s >= 2:
                    pe.wait_ge(exp_ready, s - 1)
                if s < C:
                    pe.wait_ge(maskT_ready, s + 1)
                if s == 0:
                    pe.wait_ge(v_ready, 2)
                for j in range(2):
                    mm(ps[:, EXPBANK + s % 2 * 2 + j, :], ident_b[:], maskT[:, s % C, :], stop=False)

            def score_cols(s):
                p, a = divmod(s, C)
                if a == 0:
                    pe.wait_ge(m_stacked, 2 * 16 * (p + 1))
                bank = EXPBANK + s % 2 * 2
                for j in range(2):
                    h = 2 * p + j
                    ins = mm(ps[:, bank + j, :], k_stack[0:SROWS, h, a * P:(a + 1) * P], q_stack[0:SROWS, h, :],
                             start=False)
                ins.then_inc(exp_psum, 1)

            def add_values(g, a):
                pe.wait_ge(exp_ready, (2 * g + 1) * C + a + 1)
                if g > 0 and a == 0:
                    pe.wait_ge(on_ready, g)
                for j in range(HG):
                    step = (2 * g + j // 2) * C + a
                    ins = mm(ps[HS * j:HS * (j + 1), OUTBANK, :], v[:, a, g * P + HS * j:g * P + HS * (j + 1)],
                             pT[:, step % SLOTS, j % 2, :],
                             start=(a == 0), stop=(a == C - 1), pos=(0, HS * j))
                ins.then_inc(pv_done, 1)

            def turn_outputs(g):
                pe.wait_ge(oT_ready, g + 1)
                for c in range(C):
                    ins = nc.tensor.transpose(ps[:, OUTBANK, c * P:(c + 1) * P], oT[:, c * P:(c + 1) * P], ident)
                ins.then_inc(o_psum, 1)

            def acc(l, t):
                return ps[:, ACCBANK[l] + t, :]

            def add_bias(l, t):
                for n in range(2):
                    mm(acc(l, t)[:, 0:HID], onehot[:, t * P:(t + 1) * P], bias_part[:, n, l * HID:(l + 1) * HID],
                       start=(n == 0), stop=False)

            hold_clock(KEEP_WARM)
            pe.wait_ge(k_stacked, 16 * len(BLOCKS))
            pe.wait_ge(first_low, FIRST)
            at = RING.index(("unit", 2 * UNITS - 1)) + 1
            turned_at = RING.index(("turn", 0))
            for i in range(at):
                if 0 < i - turned_at <= C:
                    values(i - turned_at - 1)
                elif i < turned_at:
                    hold_clock(1)
                fill(i)
            pe.wait_ge(ident_b_ready, 1)
            add_mask(1)
            add_mask(0)
            for s in range(STEPS + 1):
                if s < STEPS:
                    if s >= 2:
                        add_mask(s)
                    score_cols(s)
                upto = at + (FILLS[s] if s < len(FILLS) else 0)
                for i in range(at, upto):
                    fill(i)
                at = upto
                for g in range(G):
                    for a in range(C):
                        if ADD_VALUES[g][a] == s:
                            add_values(g, a)
                if s == TURN_OUTPUTS_AFTER:
                    turn_outputs(0)
                if s == PAIRS_AFTER:
                    pe.wait_ge(max_read, MP * UNITS)
                    pe.wait_ge(ones_ready, 1)
                    pe.wait_ge(past_ready, 1)
                    mm(ps[:, 1, :], ones_r[:], past[:]).then_inc(pair_psum, 1)
            turn_outputs(1)
            pe.wait_ge(onehot_ready, 1)
            pe.wait_ge(bias_ready, 1)
            for t in range(2):
                add_bias(0, t)
            pe.wait_ge(m_low, MP)
            pe.wait_ge(slot_d_ready, 1)
            mm(ps[:, 2, :], ones_r[:], slot_d[:].rearrange("p c n -> p (c n)")).then_inc(slot_r_psum, 1)
            pe.wait_ge(pair_ready, 1)
            pe.wait_ge(x_bo_ready, 1)
            mm(ps[:, 1, :], ident, x_bo[:].rearrange("p c d -> p (c d)"), stop=False)
            pe.wait_ge(on_ready, G)
            for c in range(C):
                ins = nc.tensor.transpose(ps[:, 0, c * P:(c + 1) * P], on[:, c, :], ident)
            ins.then_inc(onT_psum, 1)
            add_bias(0, 2)
            hold_clock(2, bank=3)
            pe.wait_ge(onT_ready, 1)
            for c in range(C):
                ins = mm(ps[:, 1, c * P:(c + 1) * P], onT[:, c * P:(c + 1) * P], l_("wo"), start=False)
            ins.then_inc(attn_psum, 1)
            add_bias(0, 3)
            hold_clock(NORM_WARM, bank=3)

            def turn_window(l, t):
                pe.wait_ge(h_ready, l * C + t + 1)
                for k in range(KH):
                    ins = nc.tensor.transpose(acc(l, t)[:, HID + k * P:HID + (k + 1) * P],
                                              hs[:, t, k * P:(k + 1) * P], ident)
                ins.then_inc(h_turned, 1)

            def add_pair(l, i):
                n = l * PAIRS + i
                t = window_of(mybir.EngineType.PE, i)
                if i < E and i % (E // WPARTS) == 0:
                    pe.wait_ge(w_ready[l], i // (E // WPARTS) + 1)
                pe.wait_ge(picked_ready, n + 1)
                flat = ps[:, ACCBANK[l]:ACCBANK[l] + C, :].rearrange("p b n -> p (b n)")
                for k in range(KH):
                    at = ((E - 1 - i) * KH + k) * HID
                    ins = mm(flat[:, bass.ds(t * N, HID)], picked[:, n % 3, k, :],
                             w[l][:, bass.ds(t * (KH * HID) + at, HID)], start=False, stop=(k == KH - 1))
                ins.then_inc(pair_done, 1)

            pe.wait_ge(gather_ready, 1)
            pe.wait_ge(slot_r_ready, 1)
            for n in range(2):
                for c in range(C):
                    pe.wait_ge(z_low if n else z_high, c + 1)
                    ins = mm(ps[:, 0 if n else 2, :], z_part[:, n, c, :], gather[:, c, :], start=(c == 0),
                             stop=(c == C - 1))
                ins.then_inc(zT_psum, 1)
            pe.wait_ge(zT_high, 1)
            pe.wait_ge(wi_ready, 2)
            for k in range(KH):
                for n in range(2):
                    mm(ps[:, 3 - k, :], wi_part[:, n, k * P:(k + 1) * P], zT_part[:, 0, :], start=(n == 0), stop=False)
            pe.wait_ge(zT_low, 1)
            for k in range(KH):
                mm(ps[:, 3 - k, :], wi_part[:, 0, k * P:(k + 1) * P], zT_part[:, 1, :], start=False)\
                    .then_inc(h0_psum, 1)
            pe.wait_ge(window_ready, 1)
            add_bias(1, 0)
            pe.wait_ge(x2_ready, 1)
            add_bias(1, 1)

            def unsort(t):
                for n in range(2):
                    pe.wait_ge(h_low if n else h_ready, t + 1 if n else (L - 1) * C + t + 1)
                    for k in range(KH):
                        ins = mm(ps[:, 4 + k, :], hs_part[:, n, t, k * P:(k + 1) * P], scatter[:, t, :],
                                 start=(t == 0 and n == 0), stop=(t == C - 1 and n == 1))
                        if t == C - 1 and n == 1:
                            ins.then_inc(unsorted_psum, 1)

            for l in range(L):
                last = l == L - 1
                for i in range(PAIRS):
                    add_pair(l, i)
                    if l == 0 and i == 0:
                        pe.wait_ge(h0_dve, 2)
                        add_bias(1, 2)
                        pe.wait_ge(h0_act, 2)
                        add_bias(1, 3)
                    if i >= LAST and not last:
                        turn_window(l, i - LAST)
                    if i == 0 and l > 0:
                        turn_window(l - 1, C - 1)
                    if i == LAST and last:
                        pe.wait_ge(scatter_ready, 1)
                    if i >= LAST and last:
                        unsort(i - LAST)
            unsort(C - 1)
            for c in range(C):
                pe.wait_ge(unsorted_act, c // 2 + 1)
                pe.wait_ge(unsorted_dve, c // 2 + 1)
                for k in range(KH):
                    n = int(c >= STORED[1].start)
                    at = (c - STORED[n].start) * D
                    ins = mm(ps[:, 6 + n, at:at + D], hT[L][:, k, c * P:(c + 1) * P], fwo[:, k, :],
                             start=(k == 0), stop=(k == KH - 1))
                if c + 1 == STORED[n].stop:
                    ins.then_inc(out_psum, 1)


def _pack(table, width, parts):
    packed = np.zeros((P, width), np.float32)
    for name, a in parts.items():
        lo, hi = table[name]
        packed[:, lo:hi] = a
    return packed


def _by_d(a, lo=0, hi=H):
    a = a.reshape(H, DH, -1)[lo:hi]
    return a.swapaxes(0, 1).reshape(a.shape[0] * DH, -1)


def _stacked(a):
    a = a.reshape(H, DH, -1)[:FIRST]
    return np.concatenate([a] * len(BLOCKS), axis=1)


def _head_columns(a):
    wide = np.zeros((a.shape[0], G * HG, HS), a.dtype)
    wide[:, :, :DH] = a.reshape(a.shape[0], G * HG, DH)
    return wide.reshape(a.shape[0], G * P)


def _head_bias(b):
    wide = np.zeros((G * HG, HS), b.dtype)
    wide[:, :DH] = b.reshape(G * HG, DH)
    wide[:, DH] = 1
    return wide.reshape(G * P)


def kernel(x, adj, L0_gnn_h_neigh, L0_gnn_Wq, L0_gnn_bq, L0_gnn_Wk, L0_gnn_bk, L0_gnn_Wv, L0_gnn_bv, L0_gnn_Wo,
           L0_gnn_bo, L0_gnn_E, L0_ffn_route_id, L0_ffn_Wi, L0_ffn_bi, L0_ffn_Wr, L0_ffn_br, L0_ffn_Ws, L0_ffn_bs,
           L0_ffn_Wo, L0_ffn_bo):
    import concourse.bacc as bacc
    from concourse.bass_utils import run_bass_kernel_spmd

    to = np.asarray
    rows = np.arange(P, dtype=np.float32)[:, None]
    cols = np.arange(N, dtype=np.float32)[None, :]
    wq = [_by_d(to(L0_gnn_Wq), *group) for group in GROUPS]
    early = _pack(EARLY, EARLY_W, {
        "ident": np.eye(P, dtype=np.float32),
        "wq_first": _stacked(to(L0_gnn_Wq)).reshape(FIRST * MROW, D).T, "wq": np.concatenate(wq).T,
        "hnT": to(L0_gnn_h_neigh).T, "ET": to(L0_gnn_E).T,
        "wk": _by_d(to(L0_gnn_Wk)).T, "bk": _by_d(to(L0_gnn_bk)),
    })
    lo, hi = EARLY["bq_first"]
    early[:MROW, lo:hi] = _stacked(to(L0_gnn_bq))[:, :, 0].T
    lo, hi = EARLY["bq"]
    early[:QROWS, lo:hi] = np.concatenate([_by_d(to(L0_gnn_bq), *group) for group in GROUPS])
    middle = _pack(MIDDLE, MIDDLE_W, {
        "wv": _head_columns(to(L0_gnn_Wv).T), "bv": _head_bias(to(L0_gnn_bv))[None, :],
    })
    late = _pack(LATE, LATE_W, {
        "wo": to(L0_gnn_Wo).T, "bo": to(L0_gnn_bo)[None, :],
        "iota": cols, "tile_of": cols // P,
        "row_no": rows + P * np.arange(C, dtype=np.float32), "in_group": rows % RPG,
        "group_of": rows // RPG + P // RPG * np.arange(C, dtype=np.float32),
        "cap": np.where(rows < E, 2.0 * N, (rows - E + 1) * P),
        "wi": to(L0_ffn_Wi).T, "bi": to(L0_ffn_bi).reshape(KH, P).T,
        "ws": to(L0_ffn_Ws)[:, 0].transpose(2, 0, 1).reshape(KH, P, L, HID).transpose(1, 2, 0, 3).reshape(P, -1),
        "fwo": to(L0_ffn_Wo).T.reshape(KH, P, D).transpose(1, 0, 2).reshape(P, KH * D),
        "fbo": to(L0_ffn_bo)[None, :],
    })
    route = to(L0_ffn_route_id)
    adj = to(adj)
    arrays = {
        "x": to(x), "early": early, "middle": middle, "late": late, "adj": adj, "adjT": adj.T,
        "route_tok": np.repeat(route, RPG).reshape(C, P).T, "route_row": route[None, :],
        "br": to(L0_ffn_br).transpose(1, 0, 2).reshape(E, L * HID),
        "bs": to(L0_ffn_bs).reshape(1, L * HID),
        "wr": to(L0_ffn_Wr)[:, ::-1].transpose(0, 3, 1, 2).reshape(L, KH, P, E, HID).transpose(0, 2, 3, 1, 4)
              .reshape(L, P, -1),
    }
    nc = bacc.Bacc("TRN2", target_bir_lowering=False, num_devices=1)
    given, args = {}, []
    for name, a in arrays.items():
        given[f"in_{name}"] = np.ascontiguousarray(a)
        args.append(nc.dram_tensor(f"in_{name}", a.shape, mybir.dt.from_np(a.dtype), kind="ExternalInput").ap())
    out = nc.dram_tensor("out", (N, D), F32, kind="ExternalOutput").ap()
    gnn_ffn_kernel(nc, *args, out)
    return run_bass_kernel_spmd(nc, [given], core_ids=[0]).results[0]["out"]
```
